# Optimizing a Trainium2 kernel written in Bass

```python
import numpy as np
import jax
import jax.numpy as jnp

def _softmax(x, axis=-1):
    return jax.nn.softmax(x, axis=axis)

def _gelu(x):
    return jax.nn.gelu(x, approximate=True)

def _silu(x):
    return jax.nn.silu(x)

def _sigmoid(x):
    return jax.nn.sigmoid(x)

def _layernorm(x, axis=-1, eps=1e-05):
    m = jnp.mean(x, axis=axis, keepdims=True)
    v = jnp.var(x, axis=axis, keepdims=True)
    return (x - m) / jnp.sqrt(v + eps)

def _scatter_add(tgt, idx, src, axis=0):
    return tgt.at[idx].add(src)

def _segment_sum(src, seg, n):
    return jax.ops.segment_sum(src, seg, n)
kernel_name = 'mk_seq_postln_d1_jaxref_r4_bf6818'

def setup_inputs(seed: int=0):
    np.random.seed(seed)
    _w = jnp.asarray

    def _L0_attn_setup():
        import jax, jax.numpy as jnp
        import numpy as np
        DIM = 256
        HEADS = 16
        HEAD_DIM = DIM // HEADS
        SCALE = HEAD_DIM ** (-0.5)

        def apply_rope(x, theta=10000.0):
            n, d = (x.shape[2], x.shape[3])
            seq = jnp.arange(n, dtype=jnp.float32)
            inv = 1.0 / theta ** (jnp.arange(0, d, 2, dtype=jnp.float32) / d)
            freqs = seq[:, None] * inv[None, :]
            cos = jnp.cos(freqs)[None, None]
            sin = jnp.sin(freqs)[None, None]
            x1, x2 = jnp.split(x, 2, axis=-1)
            return jnp.concatenate([x1 * cos - x2 * sin, x1 * sin + x2 * cos], axis=-1)
        key = jax.random.key(seed)
        ks = jax.random.split(key, 7)
        s = DIM ** (-0.5)
        return {'x': jax.random.normal(ks[0], (2, 512, DIM), dtype=jnp.float32), 'Wqkv': jax.random.normal(ks[1], (3 * DIM, DIM), dtype=jnp.float32) * s, 'bqkv': jax.random.normal(ks[2], (3 * DIM,), dtype=jnp.float32) * 0.02, 'Wpre': jax.random.normal(ks[3], (HEADS, HEADS), dtype=jnp.float32) * HEADS ** (-0.5), 'Wpost': jax.random.normal(ks[4], (HEADS, HEADS), dtype=jnp.float32) * HEADS ** (-0.5), 'Wout': jax.random.normal(ks[5], (DIM, DIM), dtype=jnp.float32) * s, 'bout': jax.random.normal(ks[6], (DIM,), dtype=jnp.float32) * 0.02}
    _L0_attn_in = _L0_attn_setup()

    def _L0_ffn_setup():
        import jax, jax.numpy as jnp
        import numpy as np
        LN_EPS = 1e-05
        NORM_EPS = 1e-12

        def _layernorm(x, gamma, beta):
            mu = x.mean(axis=-1, keepdims=True)
            var = ((x - mu) ** 2).mean(axis=-1, keepdims=True)
            return (x - mu) * jax.lax.rsqrt(var + LN_EPS) * gamma + beta

        def _l2norm(x, axis):
            n = jnp.sqrt((x ** 2).sum(axis=axis, keepdims=True))
            return x / jnp.maximum(n, NORM_EPS)
        key = jax.random.key(seed)
        ks = jax.random.split(key, 4)
        B, N, D, E, S, H = (64, 64, 256, 16, 16, 64)
        x = jax.random.normal(ks[0], (B, N, D), dtype=jnp.float32)
        mu = jax.random.normal(ks[1], (D, E, S), dtype=jnp.float32) / np.sqrt(D)
        w1 = jax.random.normal(ks[2], (E, D, H), dtype=jnp.float32) * np.sqrt(2.0 / D)
        w2 = jax.random.normal(ks[3], (E, H, D), dtype=jnp.float32) * np.sqrt(2.0 / (H + D))
        return {'x': x, 'ln_gamma': jnp.ones((D,), jnp.float32), 'ln_beta': jnp.zeros((D,), jnp.float32), 'mu': mu, 'scale': jnp.ones((1,), jnp.float32), 'w1': w1, 'b1': jnp.zeros((E, H), jnp.float32), 'w2': w2, 'b2': jnp.zeros((E, D), jnp.float32)}
    _L0_ffn_in = _L0_ffn_setup()
    _d = {'L0_attn_x': _L0_attn_in['x'], 'L0_attn_Wqkv': _L0_attn_in['Wqkv'], 'L0_attn_bqkv': _L0_attn_in['bqkv'], 'L0_attn_Wpre': _L0_attn_in['Wpre'], 'L0_attn_Wpost': _L0_attn_in['Wpost'], 'L0_attn_Wout': _L0_attn_in['Wout'], 'L0_attn_bout': _L0_attn_in['bout'], 'L0_ffn_ln_gamma': _L0_ffn_in['ln_gamma'], 'L0_ffn_ln_beta': _L0_ffn_in['ln_beta'], 'L0_ffn_mu': _L0_ffn_in['mu'], 'L0_ffn_scale': _L0_ffn_in['scale'], 'L0_ffn_w1': _L0_ffn_in['w1'], 'L0_ffn_b1': _L0_ffn_in['b1'], 'L0_ffn_w2': _L0_ffn_in['w2'], 'L0_ffn_b2': _L0_ffn_in['b2']}
    _x0 = _d['L0_attn_x']
    _d['L0_attn_x'] = jax.random.normal(jax.random.fold_in(jax.random.key(seed), 1), (4, 2048, 256), dtype=_x0.dtype)
    del _x0
    return _d

def reference(L0_attn_x, L0_attn_Wqkv, L0_attn_bqkv, L0_attn_Wpre, L0_attn_Wpost, L0_attn_Wout, L0_attn_bout, L0_ffn_ln_gamma, L0_ffn_ln_beta, L0_ffn_mu, L0_ffn_scale, L0_ffn_w1, L0_ffn_b1, L0_ffn_w2, L0_ffn_b2):

    def _L0_attn_ref(x, Wqkv, bqkv, Wpre, Wpost, Wout, bout):
        import jax, jax.numpy as jnp
        import numpy as np
        DIM = 256
        HEADS = 16
        HEAD_DIM = DIM // HEADS
        SCALE = HEAD_DIM ** (-0.5)

        def apply_rope(x, theta=10000.0):
            n, d = (x.shape[2], x.shape[3])
            seq = jnp.arange(n, dtype=jnp.float32)
            inv = 1.0 / theta ** (jnp.arange(0, d, 2, dtype=jnp.float32) / d)
            freqs = seq[:, None] * inv[None, :]
            cos = jnp.cos(freqs)[None, None]
            sin = jnp.sin(freqs)[None, None]
            x1, x2 = jnp.split(x, 2, axis=-1)
            return jnp.concatenate([x1 * cos - x2 * sin, x1 * sin + x2 * cos], axis=-1)
        b, n, _ = x.shape
        qkv = x @ Wqkv.T + bqkv
        q, k, v = jnp.split(qkv, 3, axis=-1)
        reshape = lambda t: t.reshape(b, n, HEADS, HEAD_DIM).transpose(0, 2, 1, 3)
        q, k, v = (reshape(q), reshape(k), reshape(v))
        q = apply_rope(q)
        k = apply_rope(k)
        logits = jnp.einsum('bhid,bhjd->bhij', q, k) * SCALE
        logits = jnp.einsum('bhij,gh->bgij', logits, Wpre)
        attn = jax.nn.softmax(logits, axis=-1)
        attn = jnp.einsum('bhij,gh->bgij', attn, Wpost)
        out = jnp.einsum('bhij,bhjd->bhid', attn, v)
        out = out.transpose(0, 2, 1, 3).reshape(b, n, DIM)
        return out @ Wout.T + bout

    def _L0_ffn_ref(x, ln_gamma, ln_beta, mu, scale, w1, b1, w2, b2):
        import jax, jax.numpy as jnp
        import numpy as np
        LN_EPS = 1e-05
        NORM_EPS = 1e-12

        def _layernorm(x, gamma, beta):
            mu = x.mean(axis=-1, keepdims=True)
            var = ((x - mu) ** 2).mean(axis=-1, keepdims=True)
            return (x - mu) * jax.lax.rsqrt(var + LN_EPS) * gamma + beta

        def _l2norm(x, axis):
            n = jnp.sqrt((x ** 2).sum(axis=axis, keepdims=True))
            return x / jnp.maximum(n, NORM_EPS)
        B, N, D = x.shape
        _, E, S = mu.shape
        xn = _layernorm(x, ln_gamma, ln_beta)
        x_unit = _l2norm(xn, axis=-1)
        mu_unit = _l2norm(mu, axis=0)
        logits = jnp.einsum('bnd,des->bnes', x_unit * scale, mu_unit)
        dispatch = jax.nn.softmax(logits, axis=1)
        combine = jax.nn.softmax(logits.reshape(B, N, E * S), axis=-1).reshape(B, N, E, S)
        slot_in = jnp.einsum('bnd,bnes->besd', xn, dispatch)
        h = jax.nn.gelu(jnp.einsum('besd,edh->besh', slot_in, w1) + b1[None, :, None, :], approximate=False)
        slot_out = jnp.einsum('besh,ehd->besd', h, w2) + b2[None, :, None, :]
        out = jnp.einsum('besd,bnes->bnd', slot_out, combine)
        return out
    x = L0_attn_x
    x = _layernorm(x + _L0_attn_ref(x, L0_attn_Wqkv, L0_attn_bqkv, L0_attn_Wpre, L0_attn_Wpost, L0_attn_Wout, L0_attn_bout), axis=-1)
    x = _layernorm(x + _L0_ffn_ref(x, L0_ffn_ln_gamma, L0_ffn_ln_beta, L0_ffn_mu, L0_ffn_scale, L0_ffn_w1, L0_ffn_b1, L0_ffn_w2, L0_ffn_b2), axis=-1)
    return x

_drawn_inputs = setup_inputs


def setup_inputs(seed=0):
    import zlib

    import numpy as np

    out = dict(_drawn_inputs(seed))
    spreads = {'L0_ffn_ln_gamma': (1.0, 0.6),
     'L0_ffn_ln_beta': (0.0, 0.726),
     'L0_ffn_b1': (0.0, 0.8),
     'L0_ffn_b2': (0.0, 0.318)}
    factors = {'L0_attn_bqkv': 3.563,
     'L0_attn_bout': 2.7,
     'L0_ffn_mu': 8.0,
     'L0_ffn_w1': 4.74,
     'L0_ffn_w2': 3.887}
    for name, (base, spread) in spreads.items():
        noise = np.random.default_rng([zlib.crc32(name.encode()), seed]).standard_normal(out[name].shape)
        drawn = base * np.exp(spread * noise) if base else spread * noise
        out[name] = jnp.asarray(drawn.astype(out[name].dtype))
    for name, factor in factors.items():
        out[name] = (out[name] * factor).astype(out[name].dtype)
    return out
```

```python
from contextlib import ExitStack

import concourse.bass as bass
from concourse import mybir
import numpy as np

F32 = mybir.dt.float32
F32R = mybir.dt.float32r
F16 = mybir.dt.float16
I32 = mybir.dt.int32
ALU = mybir.AluOpType
ACT = mybir.ActivationFunctionType
X = mybir.AxisListType.X

P = 128
B, N, DIM = 4, 2048, 256
H, HD = 16, 16
HALF = HD // 2
KT = DIM // P
QI = P // H
TI = 16
NIT = N // (TI * QI)
TG = 8
GI = TG * QI
JT = N // P
NC = 4
CW = N // NC
JC = JT // NC
GQ = H // 4
E, S, HID = 16, 16, 64
ES = E * S
EP = E // 2
PSCALE = 4096.0
LN_EPS = 1e-5
NORM_EPS2 = 1e-24
MAGIC = 1597463007.0
LOW = -3.0e38
NEWTON = 3

SLOT = dict(y=1, norm1=2, norm2=4, norm3=6, unit=8, turn=9, logits=10, keep=11, weigh=12,
            combine=13, turn_c=14, store_c=15)
POOL_LEAD = 6


def seq_layer(nc, x, xT, wqk, wv, bqk, bv, wpre, wpost, imask, wout, bout, gamma, beta, mu, scale,
              w1, b1, w2, b2, cos_t, sin_t, ident_d, out):
    ctx = ExitStack()
    with ctx:
        def sb(name, shape, dt=F32):
            return ctx.enter_context(nc.sbuf_tensor(name, shape, dt))

        def sem(name):
            return ctx.enter_context(nc.semaphore(name))

        d_x1 = nc.dram_tensor("d_x1", (B, NIT, P, DIM), F32).ap()
        d_xn = nc.dram_tensor("d_xn", (B, NIT, P, DIM), F32).ap()
        d_lg = nc.dram_tensor("d_lg", (B, NIT, P, ES), F32).ap()
        d_ct = nc.dram_tensor("d_ct", (B, NIT, P, KT, P), F32).ap()

        big = sb("big", [P, JT * H * GI])
        PT = big[:, :].rearrange("p (j g i) -> p j g i", j=JT, g=H)
        KH = sb("KH", [P, KT, N], F32R)
        KL = sb("KL", [P, KT, N], F32R)
        V = sb("V", [P, JT, DIM])
        Q = sb("Q", [P, KT, N])
        AH = sb("AH", [P, TG, KT, P], F32R)
        AL = sb("AL", [P, TG, KT, P], F32R)
        at = sb("at", [P, KT, P])
        pr = sb("pr", [P, N])
        ph = sb("ph", [P, N], F16)
        pl = sb("pl", [P, N], F16)
        rh = sb("rh", [P, P], F16)
        rl = sb("rl", [P, P], F16)
        rt = sb("rt", [P, P])
        wpre_s = sb("wpre_s", [P, H])
        wpre_q = sb("wpre_q", [P, H])
        wpost_s = sb("wpost_s", [P, H])
        imask_s = sb("imask_s", [P, QI])
        bqk_s = sb("bqk_s", [P, 4])
        bv_s = sb("bv_s", [P, DIM])
        wout_s = sb("wout_s", [P, GQ, DIM])
        bout_s = sb("bout_s", [P, DIM])
        gamma_s = sb("gamma_s", [P, DIM])
        beta_s = sb("beta_s", [P, DIM])
        scale_s = sb("scale_s", [P, 1])
        mu_s = sb("mu_s", [P, KT, ES])
        ident = sb("ident", [P, P])
        ones = sb("ones", [P, P])
        mx = sb("mx", [P, NC])
        nmax = sb("nmax", [P, 1])
        sums = sb("sums", [P, NC])
        tot = sb("tot", [P, 1])
        rec = sb("rec", [P, 1])
        rs = sb("rs", [P, 1])
        ot = sb("ot", [P, GQ, P])
        xr = sb("xr", [P, DIM])
        xb = sb("xb", [P, DIM])
        t1 = sb("t1", [P, DIM])
        x1 = sb("x1", [P, DIM])
        xn = sb("xn", [P, DIM])
        xu = sb("xu", [P, DIM])
        xuT = sb("xuT", [P, KT, P])
        lg = sb("lg", [P, ES])
        ew = sb("ew", [P, ES])
        cT = sb("cT", [P, KT, P])
        colmax = sb("colmax", [P, ES])
        st = sb("st", [P, 6])
        mv = sb("mv", [P, 2])
        va = sb("va", [P, JT])
        ya = sb("ya", [P, JT])
        za = sb("za", [P, JT])
        ia = sb("ia", [P, JT], I32)
        nrm = sb("nrm", [P, 1])
        es_ = sb("es_", [P, 1])
        er = sb("er", [P, 1])
        mv2 = sb("mv2", [P, JT, 2])
        sts = sb("sts", [P, JT, 6])
        tt = sb("tt", [P, 1])

        o = 0

        def part(n):
            nonlocal o
            v = big[:, o:o + n]
            o += n
            return v

        cos_s, sin_s = part(N), part(N)
        wqk_s = part(KT * 4 * P).rearrange("p (k f) -> p k f", k=KT)
        wv_s = part(KT * DIM).rearrange("p (k f) -> p k f", k=KT)
        xT_s = [part(KT * CW).rearrange("p (k n) -> p k n", k=KT) for _ in range(2)]
        raw = [part(4 * CW).rearrange("p (o n) -> p o n", o=4) for _ in range(2)]
        ta, tb, tc, td, kr0, kr1 = [part(CW) for _ in range(6)]
        o = 0
        XN = part(JT * (DIM + 1)).rearrange("p (r d) -> p r d", r=JT)
        LG = part(JT * ES).rearrange("p (r e) -> p r e", r=JT)
        MB = part(ES)
        si = part(KT * DIM).rearrange("p (k d) -> p k d", k=KT)
        siT = part(KT * ES).rearrange("p (k e) -> p k e", k=KT)
        dg = part(KT * P).rearrange("p (k e) -> p k e", k=KT)
        SO = part(KT * DIM).rearrange("p (k d) -> p k d", k=KT)
        HB = part(EP * S).rearrange("p (a s) -> p a s", a=EP)
        HDg = part(EP * 2 * S).rearrange("p (a s) -> p a s", a=EP)
        Qf = Q[:, :, :].rearrange("p k n -> p (k n)")
        w1_s = Qf[:, 0:KT * E * HID].rearrange("p (k e h) -> p k e h", k=KT, e=E)
        w2_s = Qf[:, KT * E * HID:KT * E * HID + EP * DIM].rearrange("p (a d) -> p a d", a=EP)
        b2_s = pr[:, 0:KT * DIM].rearrange("p (k d) -> p k d", k=KT)
        b1_s = pr[:, KT * DIM:KT * DIM + EP]
        cm = pr[:, KT * DIM + EP:KT * DIM + EP + KT]
        rslot = pr[:, KT * DIM + EP + KT:KT * DIM + EP + 2 * KT]
        X1 = V

        psS = ctx.enter_context(nc.psum_tensor("psS", [P, NC, CW], F32))
        psP = ctx.enter_context(nc.psum_tensor("psP", [P, 2, CW], F32))
        psO = ctx.enter_context(nc.psum_tensor("psO", [P, CW], F32))
        psM = ctx.enter_context(nc.psum_tensor("psM", [P, CW], F32))

        s_const = sem("s_const")
        s_setup = sem("s_setup")
        s_carry = sem("s_carry")
        s_gone = sem("s_gone")
        s_w = sem("s_w")
        s_xT = [sem("s_xT0"), sem("s_xT1")]
        s_qk = sem("s_qk")
        s_raw = sem("s_raw")
        s_v = sem("s_v")
        s_vc = sem("s_vc")
        s_rk = sem("s_rk")
        s_kh = sem("s_kh")
        s_rq = sem("s_rq")
        s_A = sem("s_A")
        s_S = sem("s_S")
        s_mx = sem("s_mx")
        s_exp = sem("s_exp")
        s_rs = sem("s_rs")
        s_ph = sem("s_ph")
        s_pl = sem("s_pl")
        s_D = sem("s_D")
        s_evD = sem("s_evD")
        s_evA = sem("s_evA")
        s_F = sem("s_F")
        s_oc = sem("s_oc")
        s_xr = sem("s_xr")
        s_xb = sem("s_xb")
        s_y = sem("s_y")
        s_dv = sem("s_dv")
        s_nw = sem("s_nw")
        s_t1 = sem("s_t1")
        s_seed = sem("s_seed")
        s_root = sem("s_root")
        s_x1 = sem("s_x1")
        s_xn = sem("s_xn")
        s_xu = sem("s_xu")
        s_xuT = sem("s_xuT")
        s_xuTc = sem("s_xuTc")
        s_L = sem("s_L")
        s_Lc = sem("s_Lc")
        s_nrm = sem("s_nrm")
        s_E = sem("s_E")
        s_C = sem("s_C")
        s_CT = sem("s_CT")
        s_CTc = sem("s_CTc")
        s_st = sem("s_st")
        s_ld = sem("s_ld")
        s_ldc = sem("s_ldc")
        s_mp = sem("s_mp")
        s_md = sem("s_md")
        s_ma = sem("s_ma")
        s_out = sem("s_out")

        FROM_ONE = [s_A, s_rs, s_pl, s_D, s_F, s_y, s_mx, s_exp, s_ph,
                    s_evD, s_evA, s_oc, s_CTc, s_t1, s_xb, s_st, s_nw]

        block = ctx.enter_context(nc.Block())

        CONSTS = [(wpre_s[:, :], wpre), (wpost_s[:, :], wpost), (imask_s[:, :], imask), (bqk_s[:, :], bqk),
                  (bv_s[:, :], bv), (wout_s[:, :, :], wout), (bout_s[:, :], bout),
                  (gamma_s[:, :], gamma), (beta_s[:, :], beta), (scale_s[:, :], scale),
                  (mu_s[:, :, :], mu), (ident[:, :], ident_d)]

        def apart(e):
            e.sem_inc(s_carry, 1)

        def barrier(e, k):
            e.drain().then_inc(s_gone, 1)
            e.wait_ge(s_gone, 5 * k)
            apart(e)

        MEET = 3

        MP_MAXT, MP_MB, MP_SLOTS = 1, 2, 3
        MP_SIT, MP_H, MP_SO = 4, 5, 6
        MP = 6 + JT
        MD_CM, MD_DG = 1, 2
        MD_MB = 3
        MD_SUB = 4
        MD_REC, MD_SI, MD_SIT, MD_HB, MD_HZ, MD_SO = 9, 10, 11, 12, 13, 14
        MD_ROW = MD_SO
        MD_OUT = MD_ROW + 2 * JT + 1 + 3 + 4 * NEWTON
        MD = MD_OUT + 4
        MA = 6

        @block.sync
        def _(sp):
            for dst, src in CONSTS:
                sp.dma_start(dst, src).then_inc(s_const, 16)
            barrier(sp, 1)
            with sp.Fori(0, B) as b:
                sp.dma_start(wqk_s, wqk).then_inc(s_w, 16)
                sp.dma_start(wv_s, wv).then_inc(s_w, 16)
                sp.dma_start(cos_s, cos_t).then_inc(s_w, 16)
                sp.dma_start(sin_s, sin_t).then_inc(s_w, 16)
                for c in range(NC):
                    if c >= 2:
                        sp.wait_ge(s_v, b * (NC * 2) + 2 * (c - 1))
                    sp.dma_start(xT_s[c % 2], xT[b][:, :, c * CW:(c + 1) * CW]).then_inc(s_xT[c % 2], 16)
                barrier(sp, b * MEET + 2)

                def row_stores(r):
                    R = b * NIT + r
                    sp.wait_ge(s_t1, R + 1)
                    sp.wait_ge(s_xb, R + 1)
                    sp.dma_start(xr[:, :], x[b][r]).then_inc(s_xr, 16)
                    sp.wait_ge(s_x1, R + 1)
                    sp.dma_start(d_x1[b][r], x1[:, :]).then_inc(s_st, 16)
                    sp.wait_ge(s_xn, R + 1)
                    sp.dma_start(d_xn[b][r], xn[:, :]).then_inc(s_st, 16)
                    sp.wait_ge(s_Lc, R + 1)
                    sp.dma_start(d_lg[b][r], lg[:, :]).then_inc(s_st, 16)
                    sp.wait_ge(s_CTc, R + 1 + 1)
                    sp.dma_start(d_ct[b][r], cT[:, :, :]).then_inc(s_st, 16)

                with sp.Fori(0, NIT) as r:
                    row_stores(r)
                sp.wait_ge(s_st, (b + 1) * (64 * NIT) + 1)
                apart(sp)
                barrier(sp, b * MEET + 3)
                sp.dma_start(LG, d_lg[b].rearrange("r p e -> p r e")).then_inc(s_ld, 16)
                sp.dma_start(XN[:, :, 0:DIM], d_xn[b].rearrange("r p d -> p r d")).then_inc(s_ld, 16)
                sp.dma_start(w1_s, w1).then_inc(s_ld, 16)
                sp.dma_start(w2_s, w2).then_inc(s_ld, 16)
                sp.dma_start(b1_s, b1).then_inc(s_ld, 16)
                sp.dma_start(b2_s, b2).then_inc(s_ld, 16)
                sp.dma_start(X1[:, :, :], d_x1[b].rearrange("r p d -> p r d")).then_inc(s_ld, 16)
                sp.wait_ge(s_mp, b * MP + MP_SLOTS)
                sp.dma_start(LG, d_ct[b].rearrange("r p k n -> p r (k n)")).then_inc(s_ldc, 16)
                for q in range(4):
                    sp.wait_ge(s_md, b * MD + MD_OUT + q + 1)
                    sp.dma_start(out[b][4 * q:4 * q + 4].rearrange("r p d -> p r d"),
                                 X1[:, 4 * q:4 * q + 4, :]).then_inc(s_out, 16)
                sp.wait_ge(s_out, (b + 1) * 64)
                apart(sp)
                barrier(sp, b * MEET + 4)

        @block.gpsimd
        def _(g):
            for s_ in FROM_ONE:
                g.sem_inc(s_, 1)
            g.memset(ones[:, :], 1.0).then_inc(s_setup, 1)
            barrier(g, 1)
            with g.Fori(0, B) as b:
                for c in range(NC):
                    n = slice(c * CW, (c + 1) * CW)
                    g.wait_ge(s_w, b * 64 + 64)
                    g.wait_ge(s_raw, b * (4 * NC) + 4 * c + 2)
                    q0, q1 = raw[c % 2][:, 0, :], raw[c % 2][:, 1, :]
                    base = b * (6 * NC) + 6 * c
                    if c >= 1:
                        g.wait_ge(s_rq, base)
                    g.tensor_tensor(tc, q0, cos_s[:, n], ALU.mult).then_inc(s_rq, 1)
                    g.tensor_tensor(td, q1, sin_s[:, n], ALU.mult).then_inc(s_rq, 1)
                    g.wait_ge(s_rq, base + 2)
                    g.tensor_tensor(Q[:, 0, n], tc, td, ALU.subtract).then_inc(s_rq, 1)
                    g.wait_ge(s_rq, base + 3)
                    g.tensor_tensor(tc, q0, sin_s[:, n], ALU.mult).then_inc(s_rq, 1)
                    g.tensor_tensor(td, q1, cos_s[:, n], ALU.mult).then_inc(s_rq, 1)
                    g.wait_ge(s_rq, base + 5)
                    g.tensor_tensor(Q[:, 1, n], tc, td, ALU.add).then_inc(s_rq, 1)
                barrier(g, b * MEET + 2)

                def premix(it, t, fresh):
                    T = (b * NIT + it) * TI + t
                    if not fresh:
                        g.wait_ge(s_S, T * NC - (TG - 1) * NC)
                    g.wait_ge(s_A, T * 3 + 1)
                    k = t % TG
                    i0 = it * (TI * QI) + t * QI
                    v = at[:, :, :].rearrange("p k (g i) -> p k g i", g=H)
                    g.tensor_tensor(v, Q[:, :, bass.ds(i0, QI)].unsqueeze(2).broadcast_to([P, KT, H, QI]),
                                    wpre_q[:, :].unsqueeze(1).unsqueeze(3).broadcast_to([P, KT, H, QI]),
                                    ALU.mult).then_inc(s_A, 1)
                    g.wait_ge(s_A, T * 3 + 1 + 1)
                    apart(g)
                    g.tensor_copy(AH[:, k, :, :], at[:, :, :]).then_inc(s_A, 1)
                    g.wait_ge(s_A, T * 3 + 2 + 1)
                    g.tensor_tensor(AL[:, k, :, :], at[:, :, :], AH[:, k, :, :].bitcast(F32),
                                    ALU.subtract).then_inc(s_A, 1)

                def add_bias(r):
                    R = b * NIT + r
                    g.wait_ge(s_xr, R * 16 + 16)
                    g.wait_ge(s_t1, R + 1)
                    g.tensor_tensor(xb[:, :], xr[:, :], bout_s[:, :], ALU.add).then_inc(s_xb, 1)

                def newton(r, k):
                    R = b * NIT + r
                    NW = 4 * NEWTON * 3
                    g.wait_ge(s_seed, R * 3 + k + 1)
                    v, y, z = va[:, 0:1], ya[:, 0:1], za[:, 0:1]
                    n = 4 * NEWTON * k
                    for m in range(NEWTON):
                        ops = [lambda: g.tensor_tensor(z, y, y, ALU.mult),
                               lambda: g.tensor_tensor(z, z, v, ALU.mult),
                               lambda: g.tensor_scalar(z, z, -0.5, 1.5, ALU.mult, ALU.add)]
                        for op in ops:
                            g.wait_ge(s_nw, R * NW + n + 1)
                            apart(g)
                            op().then_inc(s_nw, 1)
                            n += 1
                        g.wait_ge(s_nw, R * NW + n + 1)
                        g.tensor_tensor(y, y, z, ALU.mult).then_inc(s_nw, 1)
                        n += 1
                    g.wait_ge(s_nw, R * NW + n + 1)
                    apart(g)
                    if k < 2:
                        g.tensor_copy(z, y).then_inc(s_root, 1)
                    else:
                        g.tensor_tensor(z, y, scale_s[:, :], ALU.mult).then_inc(s_root, 1)

                WORK = {2: lambda r: add_bias(r), SLOT["norm1"] + POOL_LEAD: lambda r: newton(r, 0),
                        SLOT["norm2"] + POOL_LEAD: lambda r: newton(r, 1),
                        SLOT["norm3"] + POOL_LEAD: lambda r: newton(r, 2)}

                for t in range(TI):
                    premix(0, t, t < TG)
                with g.Fori(1, NIT) as it:
                    for t in range(TI):
                        premix(it, t, False)
                        if t in WORK:
                            WORK[t](it - 1)
                for t in sorted(WORK):
                    WORK[t](NIT - 1)
                barrier(g, b * MEET + 3)
                barrier(g, b * MEET + 4)

        @block.scalar
        def _(a):
            barrier(a, 1)
            with a.Fori(0, B) as b:
                for c in range(NC):
                    for f in range(4):
                        a.wait_ge(s_qk, b * (4 * NC) + 4 * c + f + 1)
                        if c >= 2:
                            a.wait_ge(s_rq, b * (6 * NC) + 6 * (c - 1))
                            a.wait_ge(s_rk, b * (8 * NC) + 8 * (c - 1))
                        a.activation(raw[c % 2][:, f, :], psS[:, f, :], ACT.Identity,
                                     bias=bqk_s[:, f:f + 1]).then_inc(s_raw, 1)
                    for k, kr in enumerate((kr0, kr1)):
                        a.wait_ge(s_rk, b * (8 * NC) + 8 * c + 3 + 3 * k)
                        a.activation(KH[:, k, c * CW:(c + 1) * CW], kr, ACT.Copy).then_inc(s_kh, 1)
                barrier(a, b * MEET + 2)

                def exps(T, c):
                    cs = slice(c * CW, (c + 1) * CW)
                    if c == 0:
                        a.wait_ge(s_mx, T * 5 + 5 + 1)
                        a.wait_ge(s_rs, T * 3 + 1)
                        a.wait_ge(s_pl, T * 2 + 1)
                    a.activation(pr[:, cs], psS[:, c, :], ACT.Exp, bias=nmax[:, 0:1], scale=1.0,
                                 accum_out=sums[:, c:c + 1]).then_inc(s_exp, 1)

                def evac(T, t, c, Gd):
                    a.wait_ge(s_D, T * NC + c + 1 + 1)
                    if t % TG == 0:
                        a.wait_ge(s_F, Gd + 1)
                    i0 = (t % TG) * QI
                    a.activation(PT[:, c * JC:(c + 1) * JC, :, i0:i0 + QI],
                                 psP[:, 1, :].rearrange("p (j g i) -> p j g i", j=JC, g=H),
                                 ACT.Copy).then_inc(s_evA, 1)

                def highs(T):
                    a.wait_ge(s_rs, T * 3 + 3 + 1)
                    a.wait_ge(s_D, T * NC + 1)
                    for h in range(2):
                        hs = slice(h * N // 2, (h + 1) * N // 2)
                        a.activation(ph[:, hs], pr[:, hs], ACT.Copy, scale=rs[:, 0:1]).then_inc(s_ph, 1)

                def out_copy(Gd, half, R):
                    a.wait_ge(s_F, Gd + 1 + 1)
                    a.wait_ge(s_y, R + 1)
                    a.activation(ot[:, :, half * GI:(half + 1) * GI],
                                 psO[:, 0:GQ * GI].rearrange("p (q i) -> p q i", q=GQ),
                                 ACT.Copy, scale=1.0 / PSCALE).then_inc(s_oc, 1)

                def turn(r):
                    R = b * NIT + r
                    a.wait_ge(s_xuT, R + 1)
                    a.activation(xuT[:, :, :], psM[:, 0:DIM].rearrange("p (k n) -> p k n", k=KT),
                                 ACT.Copy).then_inc(s_xuTc, 1)

                def weigh(r):
                    R = b * NIT + r
                    a.wait_ge(s_nrm, R + 1)
                    a.activation(ew[:, :], lg[:, :], ACT.Exp, bias=nrm[:, 0:1], scale=1.0,
                                 accum_out=es_[:, 0:1]).then_inc(s_E, 1)

                def store_c(r):
                    R = b * NIT + r
                    a.wait_ge(s_CT, R + 1)
                    a.activation(cT[:, :, :], psM[:, 0:ES].rearrange("p (k n) -> p k n", k=KT),
                                 ACT.Copy).then_inc(s_CTc, 1)

                WORK = {SLOT["turn"]: turn, SLOT["weigh"]: weigh, SLOT["store_c"]: store_c}

                def slot(it, t, first):
                    T = (b * NIT + it) * TI + t
                    G = (b * NIT + it) * 2
                    tp = (t - 1) % TI
                    Gp = G + t // TG - (1 if t % TG == 0 else 0)
                    late = not (first and t == 0)
                    exps(T, 0)
                    exps(T, 1)
                    if late:
                        evac(T - 1, tp, 1, Gp)
                    exps(T, 2)
                    exps(T, 3)
                    if late:
                        evac(T - 1, tp, 3, Gp)
                    highs(T)
                    if t % TG == 0 and late:
                        out_copy(Gp, (t // TG + 1) % 2, b * NIT + it - (1 if t == 0 else 0))

                for t in range(TI):
                    slot(0, t, True)
                with a.Fori(1, NIT) as it:
                    for t in range(TI):
                        slot(it, t, False)
                        if t in WORK:
                            WORK[t](it - 1)
                Tl = (b * NIT + NIT) * TI
                Gl = (b + 1) * (NIT * 2)
                evac(Tl - 1, TI - 1, 1, 0)
                evac(Tl - 1, TI - 1, 3, 0)
                out_copy(Gl - 1, 1, b * NIT + NIT - 1)
                for t in sorted(WORK):
                    WORK[t](NIT - 1)
                barrier(a, b * MEET + 3)

                for q in range(4):
                    a.wait_ge(s_md, b * MD + MD_SUB + q + 1)
                    v = LG[:, 4 * q:4 * q + 4, :]
                    a.activation(v, v, ACT.Exp).then_inc(s_ma, 1)
                a.wait_ge(s_md, b * MD + MD_HZ)
                for e2 in range(2):
                    rows = slice(e2 * HID, (e2 + 1) * HID)
                    a.activation(HDg[rows, :, e2 * S:(e2 + 1) * S], HB[rows, :, :], ACT.Gelu)\
                        .then_inc(s_ma, 1)
                barrier(a, b * MEET + 4)

        @block.vector
        def _(v):
            v.memset(psO[:, :], 0.0).then_inc(s_setup, 1)
            v.wait_ge(s_const, 16 * len(CONSTS))
            v.wait_ge(s_setup, 2)
            v.tensor_scalar(wpre_q[:, :], wpre_s[:, :], float(HD) ** -0.5, None, ALU.mult).then_inc(s_setup, 1)
            v.tensor_tensor(rt[:, :].rearrange("p (g i) -> p g i", g=H),
                            wpost_s[:, :].unsqueeze(2).broadcast_to([P, H, QI]),
                            imask_s[:, :].unsqueeze(1).broadcast_to([P, H, QI]), ALU.mult).then_inc(s_setup, 1)
            v.wait_ge(s_setup, 4)
            v.tensor_copy(rh[:, :], rt[:, :]).then_inc(s_setup, 1)
            v.wait_ge(s_setup, 5)
            v.tensor_tensor(rl[:, :], rt[:, :], rh[:, :], ALU.subtract).then_inc(s_setup, 1)
            sq = big[:, 0:KT * ES].rearrange("p (k e) -> p k e", k=KT)
            mv_, my, mz, mi = (big[:, 1024 + 256 * k:1280 + 256 * k] for k in range(4))
            mi = mi.bitcast(I32)
            v.tensor_tensor(sq, mu_s[:, :, :], mu_s[:, :, :], ALU.mult).then_inc(s_setup, 1)
            v.wait_ge(s_setup, 8)
            v.tensor_scalar(mv_, psM[:, 0:ES], NORM_EPS2, None, ALU.max).then_inc(s_setup, 1)
            n = 9

            def link(ins):
                nonlocal n
                ins.then_inc(s_setup, 1)
                n += 1
                v.wait_ge(s_setup, n)

            v.wait_ge(s_setup, 9)
            link(v.tensor_scalar(mi, mv_.bitcast(I32), 1, None, ALU.logical_shift_right))
            link(v.tensor_scalar(my.bitcast(I32), mi, -1.0, MAGIC, ALU.mult, ALU.add))
            for _ in range(NEWTON):
                link(v.tensor_tensor(mz, my, my, ALU.mult))
                link(v.tensor_tensor(mz, mz, mv_, ALU.mult))
                link(v.tensor_scalar(mz, mz, -0.5, 1.5, ALU.mult, ALU.add))
                link(v.tensor_tensor(my, my, mz, ALU.mult))
            link(v.tensor_tensor(mu_s[:, :, :], mu_s[:, :, :], my.unsqueeze(1).broadcast_to([P, KT, ES]), ALU.mult))
            barrier(v, 1)

            with v.Fori(0, B) as b:
                v.memset(colmax[:, :], LOW).then_inc(s_dv, 1)
                for c in range(NC):
                    n_ = slice(c * CW, (c + 1) * CW)
                    v.wait_ge(s_w, b * 64 + 64)
                    for h in range(2):
                        v.wait_ge(s_v, b * (2 * NC) + 2 * c + h + 1)
                        v.tensor_tensor(V[:, JC * c + 2 * h:JC * c + 2 * h + 2, :],
                                        psP[:, h, :].rearrange("p (j d) -> p j d", j=2),
                                        bv_s[:, :].unsqueeze(1).broadcast_to([P, 2, DIM]),
                                        ALU.add).then_inc(s_vc, 1)
                    v.wait_ge(s_raw, b * (4 * NC) + 4 * c + 4)
                    base = b * (8 * NC) + 8 * c
                    k0, k1 = raw[c % 2][:, 2, :], raw[c % 2][:, 3, :]
                    if c >= 1:
                        v.wait_ge(s_rk, base)
                    v.tensor_tensor(ta, k0, cos_s[:, n_], ALU.mult).then_inc(s_rk, 1)
                    v.tensor_tensor(tb, k1, sin_s[:, n_], ALU.mult).then_inc(s_rk, 1)
                    v.wait_ge(s_rk, base + 2)
                    v.tensor_tensor(kr0, ta, tb, ALU.subtract).then_inc(s_rk, 1)
                    v.wait_ge(s_rk, base + 3)
                    v.tensor_tensor(ta, k0, sin_s[:, n_], ALU.mult).then_inc(s_rk, 1)
                    v.tensor_tensor(tb, k1, cos_s[:, n_], ALU.mult).then_inc(s_rk, 1)
                    v.wait_ge(s_rk, base + 5)
                    v.tensor_tensor(kr1, ta, tb, ALU.add).then_inc(s_rk, 1)
                    for k, kr in enumerate((kr0, kr1)):
                        v.wait_ge(s_kh, b * (2 * NC) + 2 * c + k + 1)
                        v.wait_ge(s_rk, base + 6)
                        v.tensor_tensor(KL[:, k, n_], kr, KH[:, k, n_].bitcast(F32),
                                        ALU.subtract).then_inc(s_rk, 1)
                barrier(v, b * MEET + 2)

                def maxes(T):
                    for c in range(NC):
                        v.wait_ge(s_S, T * NC + c + 1)
                        if c == 0:
                            v.wait_ge(s_mx, T * 5 + 1)
                        v.tensor_reduce(mx[:, c:c + 1], psS[:, c, :], X, ALU.max).then_inc(s_mx, 1)
                    v.wait_ge(s_mx, T * 5 + 4 + 1)
                    v.wait_ge(s_exp, T * NC + 1)
                    v.tensor_reduce(nmax[:, 0:1], mx[:, :], X, ALU.max, negate=True).then_inc(s_mx, 1)

                def evac(T, t, c, Gd):
                    v.wait_ge(s_D, T * NC + c + 1 + 1)
                    if t % TG == 0:
                        v.wait_ge(s_F, Gd + 1)
                    i0 = (t % TG) * QI
                    v.tensor_copy(PT[:, c * JC:(c + 1) * JC, :, i0:i0 + QI],
                                  psP[:, 0, :].rearrange("p (j g i) -> p j g i", j=JC, g=H))\
                        .then_inc(s_evD, 1)

                def recip(T):
                    v.wait_ge(s_exp, T * NC + NC + 1)
                    v.wait_ge(s_ph, T * 2 + 1)
                    v.wait_ge(s_pl, T * 2 + 1)
                    v.tensor_reduce(tot[:, 0:1], sums[:, :], X, ALU.add).then_inc(s_rs, 1)
                    v.wait_ge(s_rs, T * 3 + 1 + 1)
                    v.reciprocal(rec[:, 0:1], tot[:, 0:1]).then_inc(s_rs, 1)
                    v.wait_ge(s_rs, T * 3 + 2 + 1)
                    v.tensor_scalar(rs[:, 0:1], rec[:, 0:1], PSCALE, None, ALU.mult).then_inc(s_rs, 1)

                def lows(T):
                    for h in range(2):
                        hs = slice(h * N // 2, (h + 1) * N // 2)
                        v.wait_ge(s_ph, T * 2 + h + 1 + 1)
                        if h == 0:
                            v.wait_ge(s_rs, T * 3 + 3 + 1)
                            v.wait_ge(s_D, T * NC + 1)
                        v.scalar_tensor_tensor(out=pl[:, hs], in0=pr[:, hs], scalar=rs[:, 0:1],
                                               in1=ph[:, hs], op0=ALU.mult, op1=ALU.subtract)\
                            .then_inc(s_pl, 1)

                DV = 15
                cnt = [0]

                def chain(R, ins):
                    ins.then_inc(s_dv, 1)
                    cnt[0] += 1
                    v.wait_ge(s_dv, R * DV + cnt[0] + b + 1)
                    apart(v)

                def seed(R, src, low, op):
                    chain(R, v.tensor_scalar(va[:, 0:1], src, low, None, op))
                    chain(R, v.tensor_scalar(ia[:, 0:1], va[:, 0:1].bitcast(I32), 1, None,
                                             ALU.logical_shift_right))
                    v.tensor_scalar(ya[:, 0:1].bitcast(I32), ia[:, 0:1], -1.0, MAGIC,
                                    ALU.mult, ALU.add).then_inc(s_seed, 1)

                def norm1(r):
                    R = b * NIT + r
                    cnt[0] = 0
                    v.wait_ge(s_y, R + 1 + 1)
                    v.wait_ge(s_xb, R + 1 + 1)
                    v.tensor_tensor(t1[:, :], psM[:, 0:DIM], xb[:, :], ALU.add).then_inc(s_t1, 1)
                    v.wait_ge(s_t1, R + 1 + 1)
                    chain(R, v.bn_stats(st[:, :], t1[:, :]))
                    chain(R, v.bn_aggr(mv[:, :], st[:, :]))
                    seed(R, mv[:, 1:2], LN_EPS, ALU.add)

                def norm2(r):
                    R = b * NIT + r
                    v.wait_ge(s_root, R * 3 + 1)
                    v.wait_ge(s_st, R * 64 + 1)
                    v.tensor_scalar(x1[:, :], t1[:, :], mv[:, 0:1], za[:, 0:1],
                                    ALU.subtract, ALU.mult).then_inc(s_x1, 1)
                    v.wait_ge(s_x1, R + 1)
                    chain(R, v.bn_stats(st[:, :], x1[:, :]))
                    chain(R, v.bn_aggr(mv[:, :], st[:, :]))
                    seed(R, mv[:, 1:2], LN_EPS, ALU.add)

                def norm3(r):
                    R = b * NIT + r
                    v.wait_ge(s_root, R * 3 + 2)
                    chain(R, v.tensor_scalar(t1[:, :], x1[:, :], mv[:, 0:1], za[:, 0:1],
                                             ALU.subtract, ALU.mult))
                    chain(R, v.tensor_tensor(t1[:, :], t1[:, :], gamma_s[:, :], ALU.mult))
                    v.tensor_tensor(xn[:, :], t1[:, :], beta_s[:, :], ALU.add).then_inc(s_xn, 1)
                    v.wait_ge(s_xn, R + 1)
                    chain(R, v.tensor_tensor_reduce(out=t1[:, :], in0=xn[:, :], in1=xn[:, :], scale=1.0,
                                                    scalar=0.0, op0=ALU.mult, op1=ALU.add,
                                                    accum_out=tt[:, 0:1]))
                    seed(R, tt[:, 0:1], NORM_EPS2, ALU.max)

                def unit(r):
                    R = b * NIT + r
                    v.wait_ge(s_root, R * 3 + 3)
                    v.tensor_scalar(xu[:, :], xn[:, :], za[:, 0:1], None, ALU.mult).then_inc(s_xu, 1)

                def keep(r):
                    R = b * NIT + r
                    v.wait_ge(s_L, R + 1)
                    v.tensor_copy(lg[:, :], psM[:, 0:ES]).then_inc(s_Lc, 1)
                    v.wait_ge(s_Lc, R + 1)
                    v.tensor_reduce(nrm[:, 0:1], lg[:, :], X, ALU.max, negate=True).then_inc(s_nrm, 1)
                    chain(R, v.tensor_tensor(colmax[:, :], colmax[:, :], lg[:, :], ALU.max))

                def combine(r):
                    R = b * NIT + r
                    v.wait_ge(s_E, R + 1)
                    chain(R, v.reciprocal(er[:, 0:1], es_[:, 0:1]))
                    v.tensor_scalar(ew[:, :], ew[:, :], er[:, 0:1], None, ALU.mult).then_inc(s_C, 1)

                WORK = {SLOT["norm1"]: norm1, SLOT["norm2"]: norm2, SLOT["norm3"]: norm3,
                        SLOT["unit"]: unit, SLOT["keep"]: keep, SLOT["combine"]: combine}

                def slot(it, t, first):
                    T = (b * NIT + it) * TI + t
                    G = (b * NIT + it) * 2
                    Gp = G + t // TG - (1 if t % TG == 0 else 0)
                    maxes(T)
                    if not (first and t == 0):
                        evac(T - 1, (t - 1) % TI, 0, Gp)
                        evac(T - 1, (t - 1) % TI, 2, Gp)
                    recip(T)
                    lows(T)

                for t in range(TI):
                    slot(0, t, True)
                with v.Fori(1, NIT) as it:
                    for t in range(TI):
                        slot(it, t, False)
                        if t in WORK:
                            WORK[t](it - 1)
                Tl = (b * NIT + NIT) * TI
                evac(Tl - 1, TI - 1, 0, 0)
                evac(Tl - 1, TI - 1, 2, 0)
                for t in sorted(WORK):
                    WORK[t](NIT - 1)
                assert cnt[0] == DV, cnt
                barrier(v, b * MEET + 3)

                m0 = b * MD
                v.wait_ge(s_mp, b * MP + MP_MAXT)
                v.tensor_reduce(cm, psM[:, 0:ES].rearrange("p (k n) -> p k n", k=KT), X, ALU.max).then_inc(s_md, 1)
                v.wait_ge(s_md, m0 + MD_CM)
                v.tensor_tensor(dg, ident[:, :].unsqueeze(1).broadcast_to([P, KT, P]),
                                cm.unsqueeze(2).broadcast_to([P, KT, P]), ALU.mult).then_inc(s_md, 1)
                v.wait_ge(s_mp, b * MP + MP_MB)
                v.tensor_copy(MB, psM[:, 0:ES]).then_inc(s_md, 1)
                v.wait_ge(s_md, m0 + MD_MB)
                v.wait_ge(s_ld, b * 112 + 112)
                for q in range(4):
                    w = LG[:, 4 * q:4 * q + 4, :]
                    if q == 0:
                        v.memset(XN[:, :, DIM:DIM + 1], 1.0).then_inc(s_md, 1)
                    v.tensor_tensor(w, w, MB.unsqueeze(1).broadcast_to([P, 4, ES]), ALU.subtract).then_inc(s_md, 1)
                v.wait_ge(s_mp, b * MP + MP_SLOTS)
                v.reciprocal(rslot, psS[:, 0:2, DIM:DIM + 1].rearrange("p k a -> p (k a)")).then_inc(s_md, 1)
                v.wait_ge(s_md, m0 + MD_REC)
                v.tensor_tensor(si, psS[:, 0:2, 0:DIM], rslot.unsqueeze(2).broadcast_to([P, KT, DIM]),
                                ALU.mult).then_inc(s_md, 1)
                v.wait_ge(s_mp, b * MP + MP_SIT)
                v.tensor_copy(siT, psS[:, 2, :].rearrange("p (k e) -> p k e", k=KT)).then_inc(s_md, 1)
                v.wait_ge(s_mp, b * MP + MP_H)
                v.tensor_tensor(HB, psS[:, 3, 0:EP * S].rearrange("p (a s) -> p a s", a=EP),
                                b1_s.unsqueeze(2).broadcast_to([P, EP, S]), ALU.add).then_inc(s_md, 1)
                v.memset(HDg, 0.0).then_inc(s_md, 1)
                v.wait_ge(s_mp, b * MP + MP_SO)
                v.tensor_tensor(SO, psP[:, :, 0:DIM], b2_s, ALU.add).then_inc(s_md, 1)
                for r in range(JT):
                    v.wait_ge(s_mp, b * MP + MP_SO + r + 1)
                    v.tensor_tensor(X1[:, r, :], psS[:, r % 4, 0:DIM], X1[:, r, :], ALU.add).then_inc(s_md, 1)
                    v.wait_ge(s_md, m0 + MD_ROW + 2 * r + 1)
                    v.bn_stats(sts[:, r, :], X1[:, r, :]).then_inc(s_md, 1)
                n = MD_ROW + 2 * JT
                v.wait_ge(s_md, m0 + n)
                apart(v)
                for r in range(JT):
                    last = v.bn_aggr(mv2[:, r, :], sts[:, r, :])
                last.then_inc(s_md, 1)
                n += 1
                v.wait_ge(s_md, m0 + n)
                apart(v)

                def step(ins):
                    nonlocal n
                    ins.then_inc(s_md, 1)
                    n += 1
                    v.wait_ge(s_md, m0 + n)

                step(v.tensor_scalar(va[:, :], mv2[:, :, 1], LN_EPS, None, ALU.add))
                step(v.tensor_scalar(ia[:, :], va[:, :].bitcast(I32), 1, None, ALU.logical_shift_right))
                step(v.tensor_scalar(ya[:, :].bitcast(I32), ia[:, :], -1.0, MAGIC, ALU.mult, ALU.add))
                for _ in range(NEWTON):
                    step(v.tensor_tensor(za[:, :], ya[:, :], ya[:, :], ALU.mult))
                    step(v.tensor_tensor(za[:, :], za[:, :], va[:, :], ALU.mult))
                    step(v.tensor_scalar(za[:, :], za[:, :], -0.5, 1.5, ALU.mult, ALU.add))
                    step(v.tensor_tensor(ya[:, :], ya[:, :], za[:, :], ALU.mult))
                assert n == MD_OUT, (n, MD_OUT)
                for r in range(JT):
                    done = v.tensor_scalar(X1[:, r, :], X1[:, r, :], mv2[:, r, 0:1], ya[:, r:r + 1],
                                           ALU.subtract, ALU.mult)
                    if r % 4 == 3:
                        done.then_inc(s_md, 1)
                barrier(v, b * MEET + 4)

        @block.tensor
        def _(pe):
            pe.wait_ge(s_setup, 7)
            for k in range(KT):
                mm = pe.matmul(psM[:, 0:ES], ones[:, :], big[:, k * ES:(k + 1) * ES], start=k == 0, stop=k == KT - 1)
            mm.then_inc(s_setup, 1)
            barrier(pe, 1)
            with pe.Fori(0, B) as b:
                pe.wait_ge(s_w, b * 64 + 64)
                for c in range(NC):
                    xc = xT_s[c % 2]
                    pe.wait_ge(s_xT[c % 2], b * (8 * NC) + 16 * (c // 2) + 16)
                    for f in range(4):
                        if c >= 1:
                            pe.wait_ge(s_raw, b * (4 * NC) + 4 * (c - 1) + f + 1)
                        for k in range(KT):
                            mm = pe.matmul(psS[:, f, :], wqk_s[:, k, f * P:(f + 1) * P], xc[:, k, :],
                                           start=k == 0, stop=k == KT - 1)
                        mm.then_inc(s_qk, 1)
                    for h in range(2):
                        if c >= 1:
                            pe.wait_ge(s_vc, b * (2 * NC) + 2 * (c - 1) + h + 1)
                        for j in range(2):
                            for k in range(KT):
                                j0 = (2 * h + j) * P
                                mm = pe.matmul(psP[:, h, j * DIM:(j + 1) * DIM], xc[:, k, j0:j0 + P],
                                               wv_s[:, k, :], start=k == 0, stop=k == KT - 1)
                        mm.then_inc(s_v, 1)
                barrier(pe, b * MEET + 2)

                def scores(T, t, fresh):
                    k8 = t % TG
                    pe.wait_ge(s_A, T * 3 + 3 + 1)
                    for c in range(NC):
                        if not fresh:
                            pe.wait_ge(s_exp, (T - 1) * NC + c + 1 + 1)
                        n = 0
                        for A_, K_ in ((AH, KH), (AL, KH), (AH, KL)):
                            for k in range(KT):
                                mm = pe.matmul(psS[:, c, :], A_[:, k8, k, :], K_[:, k, c * CW:(c + 1) * CW],
                                               start=n == 0, stop=n == 5)
                                n += 1
                        mm.then_inc(s_S, 1)

                def turn(T):
                    for c in range(NC):
                        if c % 2 == 0:
                            pe.wait_ge(s_pl, T * 2 + c // 2 + 1 + 1)
                        pe.wait_ge((s_evD, s_evA)[c % 2], T * 2 + c // 2 + 1)
                        for j in range(JC):
                            cs = slice((c * JC + j) * P, (c * JC + j + 1) * P)
                            o_ = psP[:, c % 2, j * P:(j + 1) * P]
                            pe.matmul(o_, ph[:, cs], rh[:, :], start=True, stop=False)
                            pe.matmul(o_, ph[:, cs], rl[:, :], start=False, stop=False)
                            mm = pe.matmul(o_, pl[:, cs], rh[:, :], start=False, stop=True)
                        mm.then_inc(s_D, 1)

                def output(Tn, Gd):
                    pe.wait_ge(s_oc, Gd + 1)
                    for c in range(NC):
                        pe.wait_ge((s_evD, s_evA)[c % 2], Tn * 2 - 1 + c // 2 + 1)
                        for j in range(c * JC, (c + 1) * JC):
                            for q in range(GQ):
                                for w in range(4):
                                    g_ = 4 * q + w
                                    mm = pe.matmul(psO[32 * w:32 * w + HD, q * GI:(q + 1) * GI],
                                                   V[:, j, g_ * HD:(g_ + 1) * HD], PT[:, j, g_, :],
                                                   start=j == 0 and q == 0, stop=j == JT - 1,
                                                   skip_group_check=True, tile_position=(0, 32 * w))
                    mm.then_inc(s_F, 1)

                def y(r):
                    R = b * NIT + r
                    pe.wait_ge(s_oc, R * 2 + 2 + 1)
                    pe.wait_ge(s_CTc, R + 1)
                    for q in range(GQ):
                        mm = pe.matmul(psM[:, 0:DIM], ot[:, q, :], wout_s[:, q, :], start=q == 0, stop=q == GQ - 1)
                    mm.then_inc(s_y, 1)

                def turn_u(r):
                    R = b * NIT + r
                    pe.wait_ge(s_xu, R + 1)
                    for k in range(KT):
                        mm = pe.transpose(psM[:, k * P:(k + 1) * P], xu[:, k * P:(k + 1) * P], ident[:, :])
                    mm.then_inc(s_xuT, 1)

                def logits(r):
                    R = b * NIT + r
                    pe.wait_ge(s_xuTc, R + 1)
                    for k in range(KT):
                        mm = pe.matmul(psM[:, 0:ES], xuT[:, k, :], mu_s[:, k, :], start=k == 0, stop=k == KT - 1)
                    mm.then_inc(s_L, 1)

                def turn_c(r):
                    R = b * NIT + r
                    pe.wait_ge(s_C, R + 1)
                    for k in range(KT):
                        mm = pe.transpose(psM[:, k * P:(k + 1) * P], ew[:, k * P:(k + 1) * P], ident[:, :])
                    mm.then_inc(s_CT, 1)

                WORK = {SLOT["y"]: y, SLOT["turn"]: turn_u, SLOT["logits"]: logits, SLOT["turn_c"]: turn_c}

                def slot(it, t, first):
                    T = (b * NIT + it) * TI + t
                    G = (b * NIT + it) * 2
                    scores(T, t, first and t == 0)
                    if not (first and t == 0):
                        turn(T - 1)
                        if t % TG == 0:
                            output(T, G + t // TG - 1)

                for t in range(TI):
                    slot(0, t, True)
                with pe.Fori(1, NIT) as it:
                    for t in range(TI):
                        slot(it, t, False)
                        if t in WORK:
                            WORK[t](it - 1)
                Tl = (b * NIT + NIT) * TI
                turn(Tl - 1)
                output(Tl, (b + 1) * (NIT * 2) - 1)
                for t in sorted(WORK):
                    WORK[t](NIT - 1)
                barrier(pe, b * MEET + 3)

                m0 = b * MP
                for k in range(KT):
                    mm = pe.transpose(psM[:, k * P:(k + 1) * P], colmax[:, k * P:(k + 1) * P], ident[:, :])
                mm.then_inc(s_mp, 1)
                pe.wait_ge(s_md, b * MD + MD_DG)
                for k in range(KT):
                    mm = pe.matmul(psM[:, k * P:(k + 1) * P], ones[:, :], dg[:, k, :], start=True, stop=True)
                mm.then_inc(s_mp, 1)
                for r in range(JT):
                    if r % 4 == 0:
                        pe.wait_ge(s_ma, b * MA + r // 4 + 1)
                    for k in range(KT):
                        mm = pe.matmul(psS[:, k, 0:DIM + 1], LG[:, r, k * P:(k + 1) * P], XN[:, r, :],
                                       start=r == 0, stop=r == JT - 1)
                mm.then_inc(s_mp, 1)
                pe.wait_ge(s_md, b * MD + MD_SI)
                for k in range(KT):
                    for h in range(KT):
                        o0 = h * ES + k * P
                        mm = pe.transpose(psS[:, 2, o0:o0 + P], si[:, k, h * P:(h + 1) * P], ident[:, :])
                mm.then_inc(s_mp, 1)
                pe.wait_ge(s_md, b * MD + MD_SIT)
                for e in range(E):
                    e2, a_ = e % 2, e // 2
                    for k in range(KT):
                        mm = pe.matmul(psS[e2 * HID:(e2 + 1) * HID, 3, a_ * S:(a_ + 1) * S],
                                       w1_s[:, k, e, :], siT[:, k, e * S:(e + 1) * S],
                                       start=k == 0, stop=k == KT - 1)
                mm.then_inc(s_mp, 1)
                pe.wait_ge(s_ma, b * MA + MA)
                for a_ in range(EP):
                    w = a_ % 4
                    mm = pe.matmul(psP[32 * w:32 * w + 32, a_ // 4, 0:DIM], HDg[:, a_, :], w2_s[:, a_, :],
                                   start=True, stop=True)
                mm.then_inc(s_mp, 1)
                pe.wait_ge(s_md, b * MD + MD_SO)
                pe.wait_ge(s_ldc, b * 16 + 16)
                for r in range(JT):
                    if r >= 4:
                        pe.wait_ge(s_md, b * MD + MD_ROW + 2 * (r - 4) + 1)
                    for k in range(KT):
                        mm = pe.matmul(psS[:, r % 4, 0:DIM], LG[:, r, k * P:(k + 1) * P], SO[:, k, :],
                                       start=k == 0, stop=k == KT - 1)
                    mm.then_inc(s_mp, 1)
                barrier(pe, b * MEET + 4)


def _tables():
    inv = (1.0 / np.float32(10000.0) ** (np.arange(0, HD, 2, dtype=np.float32) / np.float32(HD))).astype(np.float32)
    freqs = np.arange(N, dtype=np.float32)[:, None] * inv[None, :]
    both = []
    for f in (np.cos, np.sin):
        t = f(freqs.astype(np.float64)).astype(np.float32).T
        both.append(np.ascontiguousarray(np.tile(t, (H, 1))))
    return both


def kernel(**inputs):
    import concourse.bacc as bacc
    from concourse.bass_utils import run_bass_kernel_spmd as run

    a = {k[3:]: np.asarray(v) for k, v in inputs.items()}
    wq = a["attn_Wqkv"]
    order = (np.arange(H)[:, None] * HD + np.arange(HALF)[None, :]).reshape(-1)
    rows = np.concatenate([order, order + HALF, DIM + order, DIM + order + HALF])

    def halves(m):
        return m.reshape(KT, P, -1).transpose(1, 0, 2)

    def wide(v):
        return np.broadcast_to(v.reshape(1, -1), (P, v.size))

    cos_t, sin_t = _tables()
    wo = np.zeros((P, GQ, DIM), np.float32)
    wo.reshape(4, 32, GQ, DIM)[:, 0:HD] = a["attn_Wout"].T.reshape(GQ, 4, HD, DIM).transpose(1, 2, 0, 3)
    arrays = dict(
        x=a["attn_x"].reshape(B, NIT, P, DIM),
        xT=a["attn_x"].transpose(0, 2, 1).reshape(B, KT, P, N).transpose(0, 2, 1, 3),
        wqk=halves(wq[rows].T), wv=halves(wq[2 * DIM:].T),
        bqk=a["attn_bqkv"][rows].reshape(4, P).T, bv=wide(a["attn_bqkv"][2 * DIM:]),
        wpre=np.repeat(a["attn_Wpre"].T, HALF, axis=0), wpost=np.repeat(a["attn_Wpost"].T, QI, axis=0),
        imask=np.tile(np.eye(QI, dtype=np.float32), (H, 1)),
        wout=wo, bout=wide(a["attn_bout"]), gamma=wide(a["ffn_ln_gamma"]), beta=wide(a["ffn_ln_beta"]),
        mu=halves(a["ffn_mu"].reshape(DIM, ES)), scale=wide(a["ffn_scale"]),
        w1=a["ffn_w1"].transpose(1, 0, 2).reshape(KT, P, E, HID).transpose(1, 0, 2, 3),
        b1=a["ffn_b1"].reshape(EP, P).T, w2=a["ffn_w2"].reshape(EP, P, DIM).transpose(1, 0, 2),
        b2=halves(np.repeat(a["ffn_b2"], S, axis=0)),
        cos_t=cos_t, sin_t=sin_t, ident_d=np.eye(P, dtype=np.float32),
    )
    arrays = {k: np.ascontiguousarray(v) for k, v in arrays.items()}
    nc = bacc.Bacc("TRN2", target_bir_lowering=False, num_devices=1)
    args = {k: nc.dram_tensor("in_" + k, v.shape, F32, kind="ExternalInput").ap() for k, v in arrays.items()}
    out = nc.dram_tensor("out_0", (B, NIT, P, DIM), F32, kind="ExternalOutput").ap()
    seq_layer(nc, out=out, **args)
    r = run(nc, [{"in_" + k: v for k, v in arrays.items()}], core_ids=[0])
    return r.results[0]["out_0"].reshape(B, N, DIM)
```

```python
from contextlib import ExitStack

import concourse.bass as bass
from concourse import mybir
import numpy as np

F32 = mybir.dt.float32
F32R = mybir.dt.float32r
F16 = mybir.dt.float16
I32 = mybir.dt.int32
ALU = mybir.AluOpType
ACT = mybir.ActivationFunctionType
X = mybir.AxisListType.X

P = 128
B, N, DIM = 4, 2048, 256
H, HD = 16, 16
HALF = HD // 2
KT = DIM // P
QI = P // H
TI = 16
NIT = N // (TI * QI)
TG = 8
GI = TG * QI
JT = N // P
NC = 4
CW = N // NC
JC = JT // NC
GQ = H // 4
E, S, HID = 16, 16, 64
ES = E * S
EP = E // 2
PSCALE = 4096.0
LN_EPS = 1e-5
NORM_EPS2 = 1e-24
MAGIC = 1597463007.0
LOW = -3.0e38
NEWTON = 3

PE_SLOT = dict(y=2, turn_u=11, logits=12, turn_c=15)
ACT_SLOT = dict(turn_u=11, weigh=13, turn_c=15)
DVE_MID = dict(residual=3, norm1=5, norm2=7, squares=8, unit=10, keep=13, combine=14)
DVE_END = dict(stats1=3, stats2=5, shift=7, colmax=13)
POOL_SLOT = dict(bias=2, root1=9, root2=11, root3=14)


def seq_layer(nc, x, xT, wqk, wv, bqk, bv, wpre, wpost, imask, wout, bout, gamma, beta, mu, scale,
              w1, b1, w2, b2, cos_t, sin_t, ident_d, out):
    ctx = ExitStack()
    with ctx:
        def sb(name, shape, dt=F32):
            return ctx.enter_context(nc.sbuf_tensor(name, shape, dt))

        def sem(name):
            return ctx.enter_context(nc.semaphore(name))

        d_x1 = nc.dram_tensor("d_x1", (B, NIT, P, DIM), F32).ap()
        d_xn = nc.dram_tensor("d_xn", (B, NIT, P, DIM), F32).ap()
        d_lg = nc.dram_tensor("d_lg", (B, NIT, P, ES), F32).ap()
        d_ct = nc.dram_tensor("d_ct", (B, NIT, P, KT, P), F32).ap()

        big = sb("big", [P, JT * H * GI])
        PT = big[:, :].rearrange("p (j g i) -> p j g i", j=JT, g=H)
        KH = sb("KH", [P, KT, N], F32R)
        KL = sb("KL", [P, KT, N], F32R)
        V = sb("V", [P, JT, DIM])
        Q = sb("Q", [P, KT, N])
        AH = sb("AH", [P, TG, KT, P], F32R)
        AL = sb("AL", [P, TG, KT, P], F32R)
        at = sb("at", [P, KT, P])
        pr = sb("pr", [P, 2, N])
        ph = sb("ph", [P, 2, N], F16)
        pl = sb("pl", [P, 2, N], F16)
        rh = sb("rh", [P, P], F16)
        rl = sb("rl", [P, P], F16)
        rt = sb("rt", [P, P])
        wpre_s = sb("wpre_s", [P, H])
        wpre_q = sb("wpre_q", [P, H])
        wpost_s = sb("wpost_s", [P, H])
        imask_s = sb("imask_s", [P, QI])
        bqk_s = sb("bqk_s", [P, 4])
        bv_s = sb("bv_s", [P, DIM])
        wout_s = sb("wout_s", [P, GQ, DIM])
        bout_s = sb("bout_s", [P, DIM])
        gamma_s = sb("gamma_s", [P, DIM])
        beta_s = sb("beta_s", [P, DIM])
        scale_s = sb("scale_s", [P, 1])
        mu_s = sb("mu_s", [P, KT, ES])
        ident = sb("ident", [P, P])
        ones = sb("ones", [P, P])
        mx = sb("mx", [P, NC])
        nmax = sb("nmax", [P, 1])
        sums = sb("sums", [P, NC])
        tot = sb("tot", [P, 1])
        rec = sb("rec", [P, 1])
        rs = sb("rs", [P, 1])
        ot = sb("ot", [P, GQ, P])
        xr = sb("xr", [P, DIM])
        xb = sb("xb", [P, DIM])
        t1 = sb("t1", [P, DIM])
        x1 = sb("x1", [P, DIM])
        xn = sb("xn", [P, DIM])
        xu = sb("xu", [P, DIM])
        xuT = sb("xuT", [P, KT, P])
        lg = sb("lg", [P, ES])
        ew = sb("ew", [P, ES])
        cT = sb("cT", [P, KT, P])
        colmax = sb("colmax", [P, ES])
        st = sb("st", [P, 6])
        mv = sb("mv", [P, 2])
        va = sb("va", [P, JT])
        ya = sb("ya", [P, JT])
        za = sb("za", [P, JT])
        ia = sb("ia", [P, JT], I32)
        nrm = sb("nrm", [P, 1])
        es_ = sb("es_", [P, 1])
        er = sb("er", [P, 1])
        mv2 = sb("mv2", [P, JT, 2])
        sts = sb("sts", [P, JT, 6])
        tt = sb("tt", [P, 1])

        o = 0

        def part(n):
            nonlocal o
            v = big[:, o:o + n]
            o += n
            return v

        cos_s, sin_s = pr[:, 0, :], pr[:, 1, :]
        phf = ph[:, :, :].rearrange("p a n -> p (a n)").bitcast(F32)
        plf = pl[:, :, :].rearrange("p a n -> p (a n)").bitcast(F32)
        wqk_s = plf[:, 0:KT * 4 * P].rearrange("p (k f) -> p k f", k=KT)
        wv_s = plf[:, KT * 4 * P:KT * (4 * P + DIM)].rearrange("p (k f) -> p k f", k=KT)
        xT_s = [phf[:, i * KT * CW:(i + 1) * KT * CW].rearrange("p (k n) -> p k n", k=KT) for i in range(2)]
        raw = [part(4 * CW).rearrange("p (o n) -> p o n", o=4) for _ in range(2)]
        ta, tb, tc, td, kr0, kr1 = [part(CW) for _ in range(6)]
        o = 0
        XN = part(JT * (DIM + 1)).rearrange("p (r d) -> p r d", r=JT)
        LG = part(JT * ES).rearrange("p (r e) -> p r e", r=JT)
        CT = part(JT * ES).rearrange("p (r e) -> p r e", r=JT)
        MB = part(ES)
        si = part(KT * DIM).rearrange("p (k d) -> p k d", k=KT)
        siT = part(KT * ES).rearrange("p (k e) -> p k e", k=KT)
        dg = part(KT * P).rearrange("p (k e) -> p k e", k=KT)
        SO = part(KT * DIM).rearrange("p (k d) -> p k d", k=KT)
        HB = part(EP * S).rearrange("p (a s) -> p a s", a=EP)
        HDg = part(EP * 2 * S).rearrange("p (a s) -> p a s", a=EP)
        Qf = Q[:, :, :].rearrange("p k n -> p (k n)")
        w1_s = Qf[:, 0:KT * E * HID].rearrange("p (k e h) -> p k e h", k=KT, e=E)
        w2_s = Qf[:, KT * E * HID:KT * E * HID + EP * DIM].rearrange("p (a d) -> p a d", a=EP)
        b2_s = part(KT * DIM).rearrange("p (k d) -> p k d", k=KT)
        b1_s, cm, rslot = part(EP), part(KT), part(KT)
        X1 = V

        psS = ctx.enter_context(nc.psum_tensor("psS", [P, NC, CW], F32))
        psP = ctx.enter_context(nc.psum_tensor("psP", [P, 2, CW], F32))
        psO = ctx.enter_context(nc.psum_tensor("psO", [P, CW], F32))
        psM = ctx.enter_context(nc.psum_tensor("psM", [P, CW], F32))

        s_const = sem("s_const")
        s_setup = sem("s_setup")
        s_carry = sem("s_carry")
        s_gone = sem("s_gone")
        s_w = sem("s_w")
        s_xT = [sem("s_xT0"), sem("s_xT1")]
        s_qk = sem("s_qk")
        s_raw = sem("s_raw")
        s_v = sem("s_v")
        s_vc = sem("s_vc")
        s_rk = sem("s_rk")
        s_kh = sem("s_kh")
        s_rq = sem("s_rq")
        s_A = sem("s_A")
        s_S = sem("s_S")
        s_mx = sem("s_mx")
        s_exp = sem("s_exp")
        s_rs = sem("s_rs")
        s_ph = sem("s_ph")
        s_pl = sem("s_pl")
        s_D = sem("s_D")
        s_evD = sem("s_evD")
        s_evA = sem("s_evA")
        s_F = sem("s_F")
        s_oc = sem("s_oc")
        s_xr = sem("s_xr")
        s_xb = sem("s_xb")
        s_y = sem("s_y")
        s_dv = sem("s_dv")
        s_nw = sem("s_nw")
        s_t1 = sem("s_t1")
        s_seed = sem("s_seed")
        s_root = sem("s_root")
        s_x1 = sem("s_x1")
        s_xn = sem("s_xn")
        s_xu = sem("s_xu")
        s_xuT = sem("s_xuT")
        s_xuTc = sem("s_xuTc")
        s_L = sem("s_L")
        s_Lc = sem("s_Lc")
        s_nrm = sem("s_nrm")
        s_E = sem("s_E")
        s_C = sem("s_C")
        s_CT = sem("s_CT")
        s_CTc = sem("s_CTc")
        s_st = sem("s_st")
        s_ld = sem("s_ld")
        s_ldc = sem("s_ldc")
        s_mp = sem("s_mp")
        s_md = sem("s_md")
        s_ma = sem("s_ma")
        s_out = sem("s_out")

        FROM_ONE = [s_A, s_rs, s_pl, s_D, s_F, s_y, s_mx, s_exp, s_ph,
                    s_evD, s_evA, s_oc, s_CTc, s_t1, s_xb, s_st, s_nw]

        block = ctx.enter_context(nc.Block())

        CONSTS = [(wpre_s[:, :], wpre), (wpost_s[:, :], wpost), (imask_s[:, :], imask), (bqk_s[:, :], bqk),
                  (bv_s[:, :], bv), (wout_s[:, :, :], wout), (bout_s[:, :], bout),
                  (gamma_s[:, :], gamma), (beta_s[:, :], beta), (scale_s[:, :], scale),
                  (mu_s[:, :, :], mu), (ident[:, :], ident_d)]

        def apart(e):
            e.sem_inc(s_carry, 1)

        def barrier(e, k):
            e.drain().then_inc(s_gone, 1)
            e.wait_ge(s_gone, 5 * k)
            apart(e)

        MEET = 3

        MP_MAXT, MP_MB, MP_SLOTS = 1, 2, 3
        MP_SIT, MP_H, MP_SO = 4, 5, 6
        MP = 6 + JT
        MD_CM, MD_DG = 1, 2
        MD_MB = 3
        MD_SUB = 4
        MD_REC, MD_SI, MD_SIT, MD_HB, MD_HZ, MD_SO = 9, 10, 11, 12, 13, 14
        MD_ROW = MD_SO
        MD_OUT = MD_ROW + 2 * JT + 1 + 3 + 4 * NEWTON
        MD = MD_OUT + 4
        MA = 6

        @block.sync
        def _(sp):
            for dst, src in CONSTS:
                sp.dma_start(dst, src).then_inc(s_const, 16)

            def tables():
                sp.dma_start(wqk_s, wqk).then_inc(s_w, 16)
                sp.dma_start(wv_s, wv).then_inc(s_w, 16)
                sp.dma_start(cos_s, cos_t).then_inc(s_w, 16)
                sp.dma_start(sin_s, sin_t).then_inc(s_w, 16)

            tables()
            barrier(sp, 1)
            with sp.Fori(0, B) as b:
                for c in range(NC):
                    if c >= 2:
                        sp.wait_ge(s_v, b * (NC * 2) + 2 * (c - 1))
                    sp.dma_start(xT_s[c % 2], xT[b][:, :, c * CW:(c + 1) * CW]).then_inc(s_xT[c % 2], 16)
                barrier(sp, b * MEET + 2)

                def row_load(r):
                    R = b * NIT + r
                    sp.wait_ge(s_xb, R + 1)
                    sp.dma_start(xr[:, :], x[b][r]).then_inc(s_xr, 16)

                def row_stores(r):
                    R = b * NIT + r
                    sp.wait_ge(s_x1, R + 1)
                    sp.dma_start(d_x1[b][r], x1[:, :]).then_inc(s_st, 16)
                    sp.wait_ge(s_xn, R + 1)
                    sp.dma_start(d_xn[b][r], xn[:, :]).then_inc(s_st, 16)
                    sp.wait_ge(s_Lc, R + 1)
                    sp.dma_start(d_lg[b][r], lg[:, :]).then_inc(s_st, 16)
                    sp.wait_ge(s_CTc, R + 1 + 1)
                    sp.dma_start(d_ct[b][r], cT[:, :, :]).then_inc(s_st, 16)

                def moe_rows(r0, r1):
                    sp.dma_start(LG[:, r0:r1, :], d_lg[b][r0:r1].rearrange("r p e -> p r e")).then_inc(s_ld, 16)
                    sp.dma_start(XN[:, r0:r1, 0:DIM], d_xn[b][r0:r1].rearrange("r p d -> p r d")).then_inc(s_ld, 16)
                    sp.dma_start(CT[:, r0:r1, :], d_ct[b][r0:r1].rearrange("r p k n -> p r (k n)"))\
                      .then_inc(s_ldc, 16)
                    sp.dma_start(X1[:, r0:r1, :], d_x1[b][r0:r1].rearrange("r p d -> p r d")).then_inc(s_ldc, 16)

                with sp.Fori(0, NIT - 1) as r:
                    row_load(r)
                    row_stores(r)
                row_load(NIT - 1)
                tiles = (b + 1) * (NIT * TI)
                sp.wait_ge(s_F, (b + 1) * (2 * NIT) + 1)
                sp.wait_ge(s_A, tiles * 3 + 1)
                sp.wait_ge(s_st, (b + 1) * (64 * NIT) - 64 + 1)
                moe_rows(0, NIT - 1)
                sp.dma_start(w1_s, w1).then_inc(s_ld, 16)
                sp.dma_start(w2_s, w2).then_inc(s_ld, 16)
                sp.dma_start(b1_s, b1).then_inc(s_ld, 16)
                sp.dma_start(b2_s, b2).then_inc(s_ld, 16)
                row_stores(NIT - 1)
                sp.wait_ge(s_st, (b + 1) * (64 * NIT) + 1)
                apart(sp)
                moe_rows(NIT - 1, NIT)
                tables()
                barrier(sp, b * MEET + 3)
                for q in range(4):
                    sp.wait_ge(s_md, b * MD + MD_OUT + q + 1)
                    sp.dma_start(out[b][4 * q:4 * q + 4].rearrange("r p d -> p r d"),
                                 X1[:, 4 * q:4 * q + 4, :]).then_inc(s_out, 16)
                sp.wait_ge(s_out, (b + 1) * 64)
                apart(sp)
                barrier(sp, b * MEET + 4)
            sp.wait_ge(s_w, (B + 1) * 64)

        @block.gpsimd
        def _(g):
            for s_ in FROM_ONE:
                g.sem_inc(s_, 1)
            g.memset(ones[:, :], 1.0).then_inc(s_setup, 1)
            barrier(g, 1)
            with g.Fori(0, B) as b:
                for c in range(NC):
                    n = slice(c * CW, (c + 1) * CW)
                    g.wait_ge(s_w, b * 64 + 64)
                    g.wait_ge(s_raw, b * (4 * NC) + 4 * c + 2)
                    q0, q1 = raw[c % 2][:, 0, :], raw[c % 2][:, 1, :]
                    base = b * (6 * NC) + 6 * c
                    if c >= 1:
                        g.wait_ge(s_rq, base)
                    g.tensor_tensor(tc, q0, cos_s[:, n], ALU.mult).then_inc(s_rq, 1)
                    g.tensor_tensor(td, q1, sin_s[:, n], ALU.mult).then_inc(s_rq, 1)
                    g.wait_ge(s_rq, base + 2)
                    g.tensor_tensor(Q[:, 0, n], tc, td, ALU.subtract).then_inc(s_rq, 1)
                    g.wait_ge(s_rq, base + 3)
                    g.tensor_tensor(tc, q0, sin_s[:, n], ALU.mult).then_inc(s_rq, 1)
                    g.tensor_tensor(td, q1, cos_s[:, n], ALU.mult).then_inc(s_rq, 1)
                    g.wait_ge(s_rq, base + 5)
                    g.tensor_tensor(Q[:, 1, n], tc, td, ALU.add).then_inc(s_rq, 1)
                barrier(g, b * MEET + 2)

                def premix(it, t, fresh):
                    T = (b * NIT + it) * TI + t
                    if not fresh:
                        g.wait_ge(s_S, T * NC - (TG - 1) * NC)
                    g.wait_ge(s_A, T * 3 + 1)
                    k = t % TG
                    i0 = it * (TI * QI) + t * QI
                    v = at[:, :, :].rearrange("p k (g i) -> p k g i", g=H)
                    g.tensor_tensor(v, Q[:, :, bass.ds(i0, QI)].unsqueeze(2).broadcast_to([P, KT, H, QI]),
                                    wpre_q[:, :].unsqueeze(1).unsqueeze(3).broadcast_to([P, KT, H, QI]),
                                    ALU.mult).then_inc(s_A, 1)
                    g.wait_ge(s_A, T * 3 + 1 + 1)
                    apart(g)
                    g.tensor_copy(AH[:, k, :, :], at[:, :, :]).then_inc(s_A, 1)
                    g.wait_ge(s_A, T * 3 + 2 + 1)
                    g.tensor_tensor(AL[:, k, :, :], at[:, :, :], AH[:, k, :, :].bitcast(F32),
                                    ALU.subtract).then_inc(s_A, 1)

                def add_bias(r):
                    R = b * NIT + r
                    g.wait_ge(s_xr, R * 16 + 16)
                    g.wait_ge(s_t1, R + 1)
                    g.tensor_tensor(xb[:, :], xr[:, :], bout_s[:, :], ALU.add).then_inc(s_xb, 1)

                def newton(r, k):
                    R = b * NIT + r
                    NW = 4 * NEWTON * 3
                    g.wait_ge(s_seed, R * 3 + k + 1)
                    v, y, z = va[:, 0:1], ya[:, 0:1], za[:, 0:1]
                    n = 4 * NEWTON * k
                    for m in range(NEWTON):
                        ops = [lambda: g.tensor_tensor(z, y, y, ALU.mult),
                               lambda: g.tensor_tensor(z, z, v, ALU.mult),
                               lambda: g.tensor_scalar(z, z, -0.5, 1.5, ALU.mult, ALU.add)]
                        for op in ops:
                            g.wait_ge(s_nw, R * NW + n + 1)
                            apart(g)
                            op().then_inc(s_nw, 1)
                            n += 1
                        g.wait_ge(s_nw, R * NW + n + 1)
                        g.tensor_tensor(y, y, z, ALU.mult).then_inc(s_nw, 1)
                        n += 1
                    g.wait_ge(s_nw, R * NW + n + 1)
                    apart(g)
                    if k < 2:
                        g.tensor_copy(z, y).then_inc(s_root, 1)
                    else:
                        g.tensor_tensor(z, y, scale_s[:, :], ALU.mult).then_inc(s_root, 1)

                WORK = {POOL_SLOT["bias"]: add_bias, POOL_SLOT["root1"]: lambda r: newton(r, 0),
                        POOL_SLOT["root2"]: lambda r: newton(r, 1),
                        POOL_SLOT["root3"]: lambda r: newton(r, 2)}

                for t in range(TI):
                    premix(0, t, t < TG)
                with g.Fori(1, NIT) as it:
                    for t in range(TI):
                        premix(it, t, False)
                        if t in WORK:
                            WORK[t](it - 1)
                for t in sorted(WORK):
                    WORK[t](NIT - 1)
                barrier(g, b * MEET + 3)
                barrier(g, b * MEET + 4)

        @block.scalar
        def _(a):
            barrier(a, 1)
            with a.Fori(0, B) as b:
                for c in range(NC):
                    for f in range(4):
                        a.wait_ge(s_qk, b * (4 * NC) + 4 * c + f + 1)
                        if c >= 2:
                            a.wait_ge(s_rq, b * (6 * NC) + 6 * (c - 1))
                            a.wait_ge(s_rk, b * (8 * NC) + 8 * (c - 1))
                        a.activation(raw[c % 2][:, f, :], psS[:, f, :], ACT.Identity,
                                     bias=bqk_s[:, f:f + 1]).then_inc(s_raw, 1)
                    for k, kr in enumerate((kr0, kr1)):
                        a.wait_ge(s_rk, b * (8 * NC) + 8 * c + 3 + 3 * k)
                        a.activation(KH[:, k, c * CW:(c + 1) * CW], kr, ACT.Copy).then_inc(s_kh, 1)
                barrier(a, b * MEET + 2)

                def exps(T, t, c, early):
                    cs = slice(c * CW, (c + 1) * CW)
                    if c == 0:
                        a.wait_ge(s_mx, T * 5 + 5 + 1)
                        a.wait_ge(s_rs, T * 3 + 1)
                        if not early:
                            a.wait_ge(s_pl, (T - 1) * 2 + 1)
                    a.activation(pr[:, t % 2, cs], psS[:, c, :], ACT.Exp, bias=nmax[:, 0:1], scale=1.0,
                                 accum_out=sums[:, c:c + 1]).then_inc(s_exp, 1)

                def evac(T, t, c, Gd):
                    a.wait_ge(s_D, T * NC + c + 1 + 1)
                    if t % TG == 0:
                        a.wait_ge(s_F, Gd + 1)
                    i0 = (t % TG) * QI
                    a.activation(PT[:, c * JC:(c + 1) * JC, :, i0:i0 + QI],
                                 psP[:, 1, :].rearrange("p (j g i) -> p j g i", j=JC, g=H),
                                 ACT.Copy).then_inc(s_evA, 1)

                def highs(T, t, early):
                    a.wait_ge(s_rs, T * 3 + 3 + 1)
                    if not early:
                        a.wait_ge(s_D, (T - 1) * NC + 1)
                    for h in range(2):
                        hs = slice(h * N // 2, (h + 1) * N // 2)
                        a.activation(ph[:, t % 2, hs], pr[:, t % 2, hs], ACT.Copy, scale=rs[:, 0:1]).then_inc(s_ph, 1)

                def out_copy(Gd, half, R):
                    a.wait_ge(s_F, Gd + 1 + 1)
                    a.wait_ge(s_y, R + 1)
                    a.activation(ot[:, :, half * GI:(half + 1) * GI],
                                 psO[:, 0:GQ * GI].rearrange("p (q i) -> p q i", q=GQ),
                                 ACT.Copy, scale=1.0 / PSCALE).then_inc(s_oc, 1)

                def turn(r):
                    R = b * NIT + r
                    a.wait_ge(s_xuT, R + 1)
                    a.activation(xuT[:, :, :], psM[:, 0:DIM].rearrange("p (k n) -> p k n", k=KT),
                                 ACT.Copy).then_inc(s_xuTc, 1)

                def weigh(r):
                    R = b * NIT + r
                    a.wait_ge(s_nrm, R + 1)
                    a.activation(ew[:, :], lg[:, :], ACT.Exp, bias=nrm[:, 0:1], scale=1.0,
                                 accum_out=es_[:, 0:1]).then_inc(s_E, 1)

                def store_c(r):
                    R = b * NIT + r
                    a.wait_ge(s_CT, R + 1)
                    a.activation(cT[:, :, :], psM[:, 0:ES].rearrange("p (k n) -> p k n", k=KT),
                                 ACT.Copy).then_inc(s_CTc, 1)

                WORK = {ACT_SLOT["turn_u"]: turn, ACT_SLOT["weigh"]: weigh, ACT_SLOT["turn_c"]: store_c}

                def slot(it, t, first):
                    T = (b * NIT + it) * TI + t
                    early = first and t < 2
                    tp, Gp = (t - 2) % TI, (b * NIT + it) * 2 + (t - 2) // TG
                    if not early:
                        evac(T - 2, tp, 1, Gp)
                    exps(T, t, 0, early)
                    exps(T, t, 1, early)
                    exps(T, t, 2, early)
                    if not early:
                        evac(T - 2, tp, 3, Gp)
                    exps(T, t, 3, early)
                    highs(T, t, early)
                    if tp % TG == TG - 1 and not early:
                        out_copy(Gp, tp // TG, b * NIT + it - tp // TG)

                for t in range(TI):
                    slot(0, t, True)
                with a.Fori(1, NIT) as it:
                    for t in range(TI):
                        slot(it, t, False)
                        if t in WORK:
                            WORK[t](it - 1)
                Tl = (b * NIT + NIT) * TI
                Gl = (b + 1) * (NIT * 2)
                for t in (2, 1):
                    evac(Tl - t, TI - t, 1, 0)
                    evac(Tl - t, TI - t, 3, 0)
                out_copy(Gl - 1, 1, b * NIT + NIT - 1)
                for t in sorted(WORK):
                    WORK[t](NIT - 1)
                barrier(a, b * MEET + 3)

                for q in range(4):
                    a.wait_ge(s_md, b * MD + MD_SUB + q + 1)
                    v = LG[:, 4 * q:4 * q + 4, :]
                    a.activation(v, v, ACT.Exp).then_inc(s_ma, 1)
                a.wait_ge(s_md, b * MD + MD_HZ)
                for e2 in range(2):
                    rows = slice(e2 * HID, (e2 + 1) * HID)
                    a.activation(HDg[rows, :, e2 * S:(e2 + 1) * S], HB[rows, :, :], ACT.Gelu)\
                        .then_inc(s_ma, 1)
                barrier(a, b * MEET + 4)

        @block.vector
        def _(v):
            v.memset(psO[:, :], 0.0).then_inc(s_setup, 1)
            v.wait_ge(s_const, 16 * len(CONSTS))
            v.wait_ge(s_setup, 2)
            v.tensor_scalar(wpre_q[:, :], wpre_s[:, :], float(HD) ** -0.5, None, ALU.mult).then_inc(s_setup, 1)
            v.tensor_tensor(rt[:, :].rearrange("p (g i) -> p g i", g=H),
                            wpost_s[:, :].unsqueeze(2).broadcast_to([P, H, QI]),
                            imask_s[:, :].unsqueeze(1).broadcast_to([P, H, QI]), ALU.mult).then_inc(s_setup, 1)
            v.wait_ge(s_setup, 4)
            v.tensor_copy(rh[:, :], rt[:, :]).then_inc(s_setup, 1)
            v.wait_ge(s_setup, 5)
            v.tensor_tensor(rl[:, :], rt[:, :], rh[:, :], ALU.subtract).then_inc(s_setup, 1)
            sq = big[:, 0:KT * ES].rearrange("p (k e) -> p k e", k=KT)
            mv_, my, mz, mi = (big[:, 1024 + 256 * k:1280 + 256 * k] for k in range(4))
            mi = mi.bitcast(I32)
            v.tensor_tensor(sq, mu_s[:, :, :], mu_s[:, :, :], ALU.mult).then_inc(s_setup, 1)
            v.wait_ge(s_setup, 8)
            v.tensor_scalar(mv_, psM[:, 0:ES], NORM_EPS2, None, ALU.max).then_inc(s_setup, 1)
            n = 9

            def link(ins):
                nonlocal n
                ins.then_inc(s_setup, 1)
                n += 1
                v.wait_ge(s_setup, n)

            v.wait_ge(s_setup, 9)
            link(v.tensor_scalar(mi, mv_.bitcast(I32), 1, None, ALU.logical_shift_right))
            link(v.tensor_scalar(my.bitcast(I32), mi, -1.0, MAGIC, ALU.mult, ALU.add))
            for _ in range(NEWTON):
                link(v.tensor_tensor(mz, my, my, ALU.mult))
                link(v.tensor_tensor(mz, mz, mv_, ALU.mult))
                link(v.tensor_scalar(mz, mz, -0.5, 1.5, ALU.mult, ALU.add))
                link(v.tensor_tensor(my, my, mz, ALU.mult))
            link(v.tensor_tensor(mu_s[:, :, :], mu_s[:, :, :], my.unsqueeze(1).broadcast_to([P, KT, ES]), ALU.mult))
            barrier(v, 1)

            with v.Fori(0, B) as b:
                v.memset(colmax[:, :], LOW).then_inc(s_dv, 1)
                for c in range(NC):
                    n_ = slice(c * CW, (c + 1) * CW)
                    v.wait_ge(s_w, b * 64 + 64)
                    for h in range(2):
                        v.wait_ge(s_v, b * (2 * NC) + 2 * c + h + 1)
                        v.tensor_tensor(V[:, JC * c + 2 * h:JC * c + 2 * h + 2, :],
                                        psP[:, h, :].rearrange("p (j d) -> p j d", j=2),
                                        bv_s[:, :].unsqueeze(1).broadcast_to([P, 2, DIM]),
                                        ALU.add).then_inc(s_vc, 1)
                    v.wait_ge(s_raw, b * (4 * NC) + 4 * c + 4)
                    base = b * (8 * NC) + 8 * c
                    k0, k1 = raw[c % 2][:, 2, :], raw[c % 2][:, 3, :]
                    if c >= 1:
                        v.wait_ge(s_rk, base)
                    v.tensor_tensor(ta, k0, cos_s[:, n_], ALU.mult).then_inc(s_rk, 1)
                    v.tensor_tensor(tb, k1, sin_s[:, n_], ALU.mult).then_inc(s_rk, 1)
                    v.wait_ge(s_rk, base + 2)
                    v.tensor_tensor(kr0, ta, tb, ALU.subtract).then_inc(s_rk, 1)
                    v.wait_ge(s_rk, base + 3)
                    v.tensor_tensor(ta, k0, sin_s[:, n_], ALU.mult).then_inc(s_rk, 1)
                    v.tensor_tensor(tb, k1, cos_s[:, n_], ALU.mult).then_inc(s_rk, 1)
                    v.wait_ge(s_rk, base + 5)
                    v.tensor_tensor(kr1, ta, tb, ALU.add).then_inc(s_rk, 1)
                    for k, kr in enumerate((kr0, kr1)):
                        v.wait_ge(s_kh, b * (2 * NC) + 2 * c + k + 1)
                        v.wait_ge(s_rk, base + 6)
                        v.tensor_tensor(KL[:, k, n_], kr, KH[:, k, n_].bitcast(F32),
                                        ALU.subtract).then_inc(s_rk, 1)
                barrier(v, b * MEET + 2)

                def chunk_max(T, c):
                    v.wait_ge(s_S, T * NC + c + 1)
                    if c == 0:
                        v.wait_ge(s_mx, T * 5 + 1)
                    v.tensor_reduce(mx[:, c:c + 1], psS[:, c, :], X, ALU.max).then_inc(s_mx, 1)

                def tile_max(T):
                    v.wait_ge(s_mx, T * 5 + 4 + 1)
                    v.wait_ge(s_exp, T * NC + 1)
                    v.tensor_reduce(nmax[:, 0:1], mx[:, :], X, ALU.max, negate=True).then_inc(s_mx, 1)

                def evac(T, t, c, Gd):
                    v.wait_ge(s_D, T * NC + c + 1 + 1)
                    if t % TG == 0:
                        v.wait_ge(s_F, Gd + 1)
                    i0 = (t % TG) * QI
                    v.tensor_copy(PT[:, c * JC:(c + 1) * JC, :, i0:i0 + QI],
                                  psP[:, c % 2, :].rearrange("p (j g i) -> p j g i", j=JC, g=H))\
                        .then_inc(s_evD, 1)

                def recip(T):
                    v.wait_ge(s_exp, T * NC + NC + 1)
                    v.wait_ge(s_ph, T * 2 + 1)
                    v.wait_ge(s_pl, T * 2 + 1)
                    v.tensor_reduce(tot[:, 0:1], sums[:, :], X, ALU.add).then_inc(s_rs, 1)
                    v.wait_ge(s_rs, T * 3 + 1 + 1)
                    v.reciprocal(rec[:, 0:1], tot[:, 0:1]).then_inc(s_rs, 1)
                    v.wait_ge(s_rs, T * 3 + 2 + 1)
                    v.tensor_scalar(rs[:, 0:1], rec[:, 0:1], PSCALE, None, ALU.mult).then_inc(s_rs, 1)

                def low(T, t, h, early):
                    hs = slice(h * N // 2, (h + 1) * N // 2)
                    v.wait_ge(s_ph, T * 2 + h + 1 + 1)
                    if h == 0:
                        v.wait_ge(s_rs, T * 3 + 3 + 1)
                        if not early:
                            v.wait_ge(s_D, (T - 1) * NC + 1)
                    v.scalar_tensor_tensor(out=pl[:, t % 2, hs], in0=pr[:, t % 2, hs], scalar=rs[:, 0:1],
                                           in1=ph[:, t % 2, hs], op0=ALU.mult, op1=ALU.subtract)\
                        .then_inc(s_pl, 1)

                DV = 15
                cnt = [0]

                def chain(R, ins):
                    ins.then_inc(s_dv, 1)
                    cnt[0] += 1
                    v.wait_ge(s_dv, R * DV + cnt[0] + b + 1)
                    apart(v)

                def seed(R, src, low, op):
                    chain(R, v.tensor_scalar(va[:, 0:1], src, low, None, op))
                    chain(R, v.tensor_scalar(ia[:, 0:1], va[:, 0:1].bitcast(I32), 1, None,
                                             ALU.logical_shift_right))
                    v.tensor_scalar(ya[:, 0:1].bitcast(I32), ia[:, 0:1], -1.0, MAGIC,
                                    ALU.mult, ALU.add).then_inc(s_seed, 1)

                def residual(r):
                    R = b * NIT + r
                    cnt[0] = 0
                    v.wait_ge(s_y, R + 1 + 1)
                    v.wait_ge(s_xb, R + 1 + 1)
                    v.tensor_tensor(t1[:, :], psM[:, 0:DIM], xb[:, :], ALU.add).then_inc(s_t1, 1)
                    v.wait_ge(s_t1, R + 1 + 1)
                    chain(R, v.bn_stats(st[:, :], t1[:, :]))

                def stats(r):
                    R = b * NIT + r
                    chain(R, v.bn_aggr(mv[:, :], st[:, :]))
                    seed(R, mv[:, 1:2], LN_EPS, ALU.add)

                def norm1(r):
                    R = b * NIT + r
                    v.wait_ge(s_root, R * 3 + 1)
                    v.wait_ge(s_st, R * 64 + 1)
                    v.tensor_scalar(x1[:, :], t1[:, :], mv[:, 0:1], za[:, 0:1],
                                    ALU.subtract, ALU.mult).then_inc(s_x1, 1)
                    v.wait_ge(s_x1, R + 1)
                    chain(R, v.bn_stats(st[:, :], x1[:, :]))

                def norm2(r):
                    R = b * NIT + r
                    v.wait_ge(s_root, R * 3 + 2)
                    chain(R, v.tensor_scalar(t1[:, :], x1[:, :], mv[:, 0:1], za[:, 0:1],
                                             ALU.subtract, ALU.mult))
                    chain(R, v.tensor_tensor(t1[:, :], t1[:, :], gamma_s[:, :], ALU.mult))

                def shift(r):
                    R = b * NIT + r
                    v.tensor_tensor(xn[:, :], t1[:, :], beta_s[:, :], ALU.add).then_inc(s_xn, 1)

                def squares(r):
                    R = b * NIT + r
                    v.wait_ge(s_xn, R + 1)
                    chain(R, v.tensor_tensor_reduce(out=t1[:, :], in0=xn[:, :], in1=xn[:, :], scale=1.0,
                                                    scalar=0.0, op0=ALU.mult, op1=ALU.add,
                                                    accum_out=tt[:, 0:1]))
                    seed(R, tt[:, 0:1], NORM_EPS2, ALU.max)

                def unit(r):
                    R = b * NIT + r
                    v.wait_ge(s_root, R * 3 + 3)
                    v.tensor_scalar(xu[:, :], xn[:, :], za[:, 0:1], None, ALU.mult).then_inc(s_xu, 1)

                def keep(r):
                    R = b * NIT + r
                    v.wait_ge(s_L, R + 1)
                    v.tensor_copy(lg[:, :], psM[:, 0:ES]).then_inc(s_Lc, 1)
                    v.wait_ge(s_Lc, R + 1)
                    v.tensor_reduce(nrm[:, 0:1], lg[:, :], X, ALU.max, negate=True).then_inc(s_nrm, 1)

                def column(r):
                    R = b * NIT + r
                    chain(R, v.tensor_tensor(colmax[:, :], colmax[:, :], lg[:, :], ALU.max))

                def combine(r):
                    R = b * NIT + r
                    v.wait_ge(s_E, R + 1)
                    chain(R, v.reciprocal(er[:, 0:1], es_[:, 0:1]))
                    v.tensor_scalar(ew[:, :], ew[:, :], er[:, 0:1], None, ALU.mult).then_inc(s_C, 1)

                MID = {DVE_MID["residual"]: residual, DVE_MID["norm1"]: norm1, DVE_MID["norm2"]: norm2,
                       DVE_MID["squares"]: squares, DVE_MID["unit"]: unit, DVE_MID["keep"]: keep,
                       DVE_MID["combine"]: combine}
                END = {DVE_END["stats1"]: stats, DVE_END["stats2"]: stats, DVE_END["shift"]: shift,
                       DVE_END["colmax"]: column}

                def slot(it, t, first, work, last=False):
                    T = (b * NIT + it) * TI + t
                    tp, Gp = (t - 2) % TI, (b * NIT + it) * 2 + (t - 2) // TG
                    if not (first and t < 2):
                        evac(T - 2, tp, 0, Gp)
                    chunk_max(T, 3)
                    tile_max(T)
                    if not (first and t < 1):
                        low(T - 1, (t - 1) % TI, 0, first and t < 3)
                    if not (first and t < 2):
                        evac(T - 2, tp, 2, Gp)
                    if work is not None and t in MID:
                        MID[t](work)
                    if not (first and t < 1):
                        low(T - 1, (t - 1) % TI, 1, first and t < 3)
                    if not last:
                        chunk_max(T + 1, 0)
                    recip(T)
                    if not last:
                        chunk_max(T + 1, 1)
                        chunk_max(T + 1, 2)
                    if work is not None and t in END:
                        END[t](work)

                for c in range(NC - 1):
                    chunk_max(b * (NIT * TI), c)
                for t in range(TI):
                    slot(0, t, True, None)
                with v.Fori(1, NIT - 1) as it:
                    for t in range(TI):
                        slot(it, t, False, it - 1)
                for t in range(TI):
                    slot(NIT - 1, t, False, NIT - 2, last=t == TI - 1)
                Tl = (b * NIT + NIT) * TI
                low(Tl - 1, TI - 1, 0, False)
                low(Tl - 1, TI - 1, 1, False)
                for t in (2, 1):
                    evac(Tl - t, TI - t, 0, 0)
                    evac(Tl - t, TI - t, 2, 0)
                for t in range(TI):
                    for steps in (MID, END):
                        if t in steps:
                            steps[t](NIT - 1)
                assert cnt[0] == DV, cnt
                barrier(v, b * MEET + 3)

                m0 = b * MD
                v.wait_ge(s_mp, b * MP + MP_MAXT)
                v.tensor_reduce(cm, psM[:, 0:ES].rearrange("p (k n) -> p k n", k=KT), X, ALU.max).then_inc(s_md, 1)
                v.wait_ge(s_md, m0 + MD_CM)
                v.tensor_tensor(dg, ident[:, :].unsqueeze(1).broadcast_to([P, KT, P]),
                                cm.unsqueeze(2).broadcast_to([P, KT, P]), ALU.mult).then_inc(s_md, 1)
                v.wait_ge(s_mp, b * MP + MP_MB)
                v.tensor_copy(MB, psM[:, 0:ES]).then_inc(s_md, 1)
                v.wait_ge(s_md, m0 + MD_MB)
                v.wait_ge(s_ld, b * 128 + 128)
                for q in range(4):
                    w = LG[:, 4 * q:4 * q + 4, :]
                    if q == 0:
                        v.memset(XN[:, :, DIM:DIM + 1], 1.0).then_inc(s_md, 1)
                    v.tensor_tensor(w, w, MB.unsqueeze(1).broadcast_to([P, 4, ES]), ALU.subtract).then_inc(s_md, 1)
                v.wait_ge(s_mp, b * MP + MP_SLOTS)
                v.reciprocal(rslot, psS[:, 0:2, DIM:DIM + 1].rearrange("p k a -> p (k a)")).then_inc(s_md, 1)
                v.wait_ge(s_md, m0 + MD_REC)
                v.tensor_tensor(si, psS[:, 0:2, 0:DIM], rslot.unsqueeze(2).broadcast_to([P, KT, DIM]),
                                ALU.mult).then_inc(s_md, 1)
                v.wait_ge(s_mp, b * MP + MP_SIT)
                v.tensor_copy(siT, psS[:, 2, :].rearrange("p (k e) -> p k e", k=KT)).then_inc(s_md, 1)
                v.wait_ge(s_mp, b * MP + MP_H)
                v.tensor_tensor(HB, psS[:, 3, 0:EP * S].rearrange("p (a s) -> p a s", a=EP),
                                b1_s.unsqueeze(2).broadcast_to([P, EP, S]), ALU.add).then_inc(s_md, 1)
                v.memset(HDg, 0.0).then_inc(s_md, 1)
                v.wait_ge(s_mp, b * MP + MP_SO)
                v.tensor_tensor(SO, psP[:, :, 0:DIM], b2_s, ALU.add).then_inc(s_md, 1)
                v.wait_ge(s_ldc, b * 64 + 64)
                for r in range(JT):
                    v.wait_ge(s_mp, b * MP + MP_SO + r + 1)
                    v.tensor_tensor(X1[:, r, :], psS[:, r % 4, 0:DIM], X1[:, r, :], ALU.add).then_inc(s_md, 1)
                    v.wait_ge(s_md, m0 + MD_ROW + 2 * r + 1)
                    v.bn_stats(sts[:, r, :], X1[:, r, :]).then_inc(s_md, 1)
                n = MD_ROW + 2 * JT
                v.wait_ge(s_md, m0 + n)
                apart(v)
                for r in range(JT):
                    last = v.bn_aggr(mv2[:, r, :], sts[:, r, :])
                last.then_inc(s_md, 1)
                n += 1
                v.wait_ge(s_md, m0 + n)
                apart(v)

                def step(ins):
                    nonlocal n
                    ins.then_inc(s_md, 1)
                    n += 1
                    v.wait_ge(s_md, m0 + n)

                step(v.tensor_scalar(va[:, :], mv2[:, :, 1], LN_EPS, None, ALU.add))
                step(v.tensor_scalar(ia[:, :], va[:, :].bitcast(I32), 1, None, ALU.logical_shift_right))
                step(v.tensor_scalar(ya[:, :].bitcast(I32), ia[:, :], -1.0, MAGIC, ALU.mult, ALU.add))
                for _ in range(NEWTON):
                    step(v.tensor_tensor(za[:, :], ya[:, :], ya[:, :], ALU.mult))
                    step(v.tensor_tensor(za[:, :], za[:, :], va[:, :], ALU.mult))
                    step(v.tensor_scalar(za[:, :], za[:, :], -0.5, 1.5, ALU.mult, ALU.add))
                    step(v.tensor_tensor(ya[:, :], ya[:, :], za[:, :], ALU.mult))
                assert n == MD_OUT, (n, MD_OUT)
                for r in range(JT):
                    done = v.tensor_scalar(X1[:, r, :], X1[:, r, :], mv2[:, r, 0:1], ya[:, r:r + 1],
                                           ALU.subtract, ALU.mult)
                    if r % 4 == 3:
                        done.then_inc(s_md, 1)
                barrier(v, b * MEET + 4)

        @block.tensor
        def _(pe):
            pe.wait_ge(s_setup, 7)
            for k in range(KT):
                mm = pe.matmul(psM[:, 0:ES], ones[:, :], big[:, k * ES:(k + 1) * ES], start=k == 0, stop=k == KT - 1)
            mm.then_inc(s_setup, 1)
            barrier(pe, 1)
            with pe.Fori(0, B) as b:
                pe.wait_ge(s_w, b * 64 + 64)
                for c in range(NC):
                    xc = xT_s[c % 2]
                    pe.wait_ge(s_xT[c % 2], b * (8 * NC) + 16 * (c // 2) + 16)
                    for f in range(4):
                        if c >= 1:
                            pe.wait_ge(s_raw, b * (4 * NC) + 4 * (c - 1) + f + 1)
                        for k in range(KT):
                            mm = pe.matmul(psS[:, f, :], wqk_s[:, k, f * P:(f + 1) * P], xc[:, k, :],
                                           start=k == 0, stop=k == KT - 1)
                        mm.then_inc(s_qk, 1)
                    for h in range(2):
                        if c >= 1:
                            pe.wait_ge(s_vc, b * (2 * NC) + 2 * (c - 1) + h + 1)
                        for j in range(2):
                            for k in range(KT):
                                j0 = (2 * h + j) * P
                                mm = pe.matmul(psP[:, h, j * DIM:(j + 1) * DIM], xc[:, k, j0:j0 + P],
                                               wv_s[:, k, :], start=k == 0, stop=k == KT - 1)
                        mm.then_inc(s_v, 1)
                barrier(pe, b * MEET + 2)

                def scores(T, t, c, fresh):
                    k8 = t % TG
                    if c == 0:
                        pe.wait_ge(s_A, T * 3 + 3 + 1)
                    if not fresh:
                        pe.wait_ge(s_exp, (T - 1) * NC + c + 1 + 1)
                    n = 0
                    for A_, K_ in ((AH, KH), (AL, KH), (AH, KL)):
                        for k in range(KT):
                            mm = pe.matmul(psS[:, c, :], A_[:, k8, k, :], K_[:, k, c * CW:(c + 1) * CW],
                                           start=n == 0, stop=n == 5)
                            n += 1
                    mm.then_inc(s_S, 1)

                def turn(T, t, c):
                    if c % 2 == 0:
                        pe.wait_ge(s_pl, T * 2 + c // 2 + 1 + 1)
                    pe.wait_ge((s_evD, s_evA)[c % 2], T * 2 + c // 2 + 1)
                    for j in range(JC):
                        cs = slice((c * JC + j) * P, (c * JC + j + 1) * P)
                        o_ = psP[:, c % 2, j * P:(j + 1) * P]
                        pe.matmul(o_, ph[:, t % 2, cs], rh[:, :], start=True, stop=False)
                        pe.matmul(o_, ph[:, t % 2, cs], rl[:, :], start=False, stop=False)
                        mm = pe.matmul(o_, pl[:, t % 2, cs], rh[:, :], start=False, stop=True)
                    mm.then_inc(s_D, 1)

                def output(Tn, Gd):
                    pe.wait_ge(s_oc, Gd + 1)
                    for c in range(NC):
                        pe.wait_ge((s_evD, s_evA)[c % 2], Tn * 2 - 1 + c // 2 + 1)
                        for j in range(c * JC, (c + 1) * JC):
                            for q in range(GQ):
                                for w in range(4):
                                    g_ = 4 * q + w
                                    mm = pe.matmul(psO[32 * w:32 * w + HD, q * GI:(q + 1) * GI],
                                                   V[:, j, g_ * HD:(g_ + 1) * HD], PT[:, j, g_, :],
                                                   start=j == 0 and q == 0, stop=j == JT - 1,
                                                   skip_group_check=True, tile_position=(0, 32 * w))
                    mm.then_inc(s_F, 1)

                def y(r):
                    R = b * NIT + r
                    pe.wait_ge(s_oc, R * 2 + 2 + 1)
                    pe.wait_ge(s_CTc, R + 1)
                    for q in range(GQ):
                        mm = pe.matmul(psM[:, 0:DIM], ot[:, q, :], wout_s[:, q, :], start=q == 0, stop=q == GQ - 1)
                    mm.then_inc(s_y, 1)

                def turn_u(r):
                    R = b * NIT + r
                    pe.wait_ge(s_xu, R + 1)
                    for k in range(KT):
                        mm = pe.transpose(psM[:, k * P:(k + 1) * P], xu[:, k * P:(k + 1) * P], ident[:, :])
                    mm.then_inc(s_xuT, 1)

                def logits(r):
                    R = b * NIT + r
                    pe.wait_ge(s_xuTc, R + 1)
                    for k in range(KT):
                        mm = pe.matmul(psM[:, 0:ES], xuT[:, k, :], mu_s[:, k, :], start=k == 0, stop=k == KT - 1)
                    mm.then_inc(s_L, 1)

                def turn_c(r):
                    R = b * NIT + r
                    pe.wait_ge(s_C, R + 1)
                    for k in range(KT):
                        mm = pe.transpose(psM[:, k * P:(k + 1) * P], ew[:, k * P:(k + 1) * P], ident[:, :])
                    mm.then_inc(s_CT, 1)

                WORK = {PE_SLOT["y"]: y, PE_SLOT["turn_u"]: turn_u, PE_SLOT["logits"]: logits,
                        PE_SLOT["turn_c"]: turn_c}

                def slot(it, t, first):
                    T = (b * NIT + it) * TI + t
                    G = (b * NIT + it) * 2
                    for c in range(NC - 1):
                        scores(T, t, c, first and t == 0)
                    if not (first and t < 2):
                        turn(T - 2, t, 0)
                    scores(T, t, NC - 1, first and t == 0)
                    if not (first and t < 2):
                        for c in range(1, NC):
                            turn(T - 2, t, c)
                        if (t - 1) % TG == 0:
                            output(T - 1, G + (t - 2) // TG)

                for t in range(TI):
                    slot(0, t, True)
                with pe.Fori(1, NIT) as it:
                    for t in range(TI):
                        slot(it, t, False)
                        if t in WORK:
                            WORK[t](it - 1)
                Tl = (b * NIT + NIT) * TI
                for t in range(2):
                    for c in range(NC):
                        turn(Tl - 2 + t, t, c)
                output(Tl, (b + 1) * (NIT * 2) - 1)
                for t in sorted(WORK):
                    WORK[t](NIT - 1)
                barrier(pe, b * MEET + 3)

                m0 = b * MP
                for k in range(KT):
                    mm = pe.transpose(psM[:, k * P:(k + 1) * P], colmax[:, k * P:(k + 1) * P], ident[:, :])
                mm.then_inc(s_mp, 1)
                pe.wait_ge(s_md, b * MD + MD_DG)
                for k in range(KT):
                    mm = pe.matmul(psM[:, k * P:(k + 1) * P], ones[:, :], dg[:, k, :], start=True, stop=True)
                mm.then_inc(s_mp, 1)
                for r in range(JT):
                    if r % 4 == 0:
                        pe.wait_ge(s_ma, b * MA + r // 4 + 1)
                    for k in range(KT):
                        mm = pe.matmul(psS[:, k, 0:DIM + 1], LG[:, r, k * P:(k + 1) * P], XN[:, r, :],
                                       start=r == 0, stop=r == JT - 1)
                mm.then_inc(s_mp, 1)
                pe.wait_ge(s_md, b * MD + MD_SI)
                for k in range(KT):
                    for h in range(KT):
                        o0 = h * ES + k * P
                        mm = pe.transpose(psS[:, 2, o0:o0 + P], si[:, k, h * P:(h + 1) * P], ident[:, :])
                mm.then_inc(s_mp, 1)
                pe.wait_ge(s_md, b * MD + MD_SIT)
                for e in range(E):
                    e2, a_ = e % 2, e // 2
                    for k in range(KT):
                        mm = pe.matmul(psS[e2 * HID:(e2 + 1) * HID, 3, a_ * S:(a_ + 1) * S],
                                       w1_s[:, k, e, :], siT[:, k, e * S:(e + 1) * S],
                                       start=k == 0, stop=k == KT - 1)
                mm.then_inc(s_mp, 1)
                pe.wait_ge(s_ma, b * MA + MA)
                for a_ in range(EP):
                    w = a_ % 4
                    mm = pe.matmul(psP[32 * w:32 * w + 32, a_ // 4, 0:DIM], HDg[:, a_, :], w2_s[:, a_, :],
                                   start=True, stop=True)
                mm.then_inc(s_mp, 1)
                pe.wait_ge(s_md, b * MD + MD_SO)
                pe.wait_ge(s_ldc, b * 64 + 64)
                for r in range(JT):
                    if r >= 4:
                        pe.wait_ge(s_md, b * MD + MD_ROW + 2 * (r - 4) + 1)
                    for k in range(KT):
                        mm = pe.matmul(psS[:, r % 4, 0:DIM], CT[:, r, k * P:(k + 1) * P], SO[:, k, :],
                                       start=k == 0, stop=k == KT - 1)
                    mm.then_inc(s_mp, 1)
                barrier(pe, b * MEET + 4)


def _tables():
    inv = (1.0 / np.float32(10000.0) ** (np.arange(0, HD, 2, dtype=np.float32) / np.float32(HD))).astype(np.float32)
    freqs = np.arange(N, dtype=np.float32)[:, None] * inv[None, :]
    both = []
    for f in (np.cos, np.sin):
        t = f(freqs.astype(np.float64)).astype(np.float32).T
        both.append(np.ascontiguousarray(np.tile(t, (H, 1))))
    return both


def kernel(**inputs):
    import concourse.bacc as bacc
    from concourse.bass_utils import run_bass_kernel_spmd as run

    a = {k[3:]: np.asarray(v) for k, v in inputs.items()}
    wq = a["attn_Wqkv"]
    order = (np.arange(H)[:, None] * HD + np.arange(HALF)[None, :]).reshape(-1)
    rows = np.concatenate([order, order + HALF, DIM + order, DIM + order + HALF])

    def halves(m):
        return m.reshape(KT, P, -1).transpose(1, 0, 2)

    def wide(v):
        return np.broadcast_to(v.reshape(1, -1), (P, v.size))

    cos_t, sin_t = _tables()
    wo = np.zeros((P, GQ, DIM), np.float32)
    wo.reshape(4, 32, GQ, DIM)[:, 0:HD] = a["attn_Wout"].T.reshape(GQ, 4, HD, DIM).transpose(1, 2, 0, 3)
    arrays = dict(
        x=a["attn_x"].reshape(B, NIT, P, DIM),
        xT=a["attn_x"].transpose(0, 2, 1).reshape(B, KT, P, N).transpose(0, 2, 1, 3),
        wqk=halves(wq[rows].T), wv=halves(wq[2 * DIM:].T),
        bqk=a["attn_bqkv"][rows].reshape(4, P).T, bv=wide(a["attn_bqkv"][2 * DIM:]),
        wpre=np.repeat(a["attn_Wpre"].T, HALF, axis=0), wpost=np.repeat(a["attn_Wpost"].T, QI, axis=0),
        imask=np.tile(np.eye(QI, dtype=np.float32), (H, 1)),
        wout=wo, bout=wide(a["attn_bout"]), gamma=wide(a["ffn_ln_gamma"]), beta=wide(a["ffn_ln_beta"]),
        mu=halves(a["ffn_mu"].reshape(DIM, ES)), scale=wide(a["ffn_scale"]),
        w1=a["ffn_w1"].transpose(1, 0, 2).reshape(KT, P, E, HID).transpose(1, 0, 2, 3),
        b1=a["ffn_b1"].reshape(EP, P).T, w2=a["ffn_w2"].reshape(EP, P, DIM).transpose(1, 0, 2),
        b2=halves(np.repeat(a["ffn_b2"], S, axis=0)),
        cos_t=cos_t, sin_t=sin_t, ident_d=np.eye(P, dtype=np.float32),
    )
    arrays = {k: np.ascontiguousarray(v) for k, v in arrays.items()}
    nc = bacc.Bacc("TRN2", target_bir_lowering=False, num_devices=1)
    args = {k: nc.dram_tensor("in_" + k, v.shape, F32, kind="ExternalInput").ap() for k, v in arrays.items()}
    out = nc.dram_tensor("out_0", (B, NIT, P, DIM), F32, kind="ExternalOutput").ap()
    seq_layer(nc, out=out, **args)
    r = run(nc, [{"in_" + k: v for k, v in arrays.items()}], core_ids=[0])
    return r.results[0]["out_0"].reshape(B, N, DIM)
```

```python
from contextlib import ExitStack

import concourse.bass as bass
from concourse import mybir
import numpy as np

F32 = mybir.dt.float32
F32R = mybir.dt.float32r
F16 = mybir.dt.float16
I32 = mybir.dt.int32
ALU = mybir.AluOpType
ACT = mybir.ActivationFunctionType
X = mybir.AxisListType.X

P = 128
B, N, DIM = 4, 2048, 256
H, HD = 16, 16
HALF = HD // 2
KT = DIM // P
QI = P // H
TI = 16
NIT = N // (TI * QI)
TG = 8
GI = TG * QI
JT = N // P
NC = 4
CW = N // NC
JC = JT // NC
LC = 3
NL = LC * CW
N2 = N // 2
GQ = H // 4
E, S, HID = 16, 16, 64
ES = E * S
EP = E // 2
PSCALE = 1024.0
LN_EPS = 1e-5
NORM_EPS2 = 1e-24
MAGIC = 1597463007.0
LOW = -3.0e38
NEWTON = 3

LAG = (2, 2, 2, 3)
EXPS = (1, 2, 3, 0)
ORDER = (("scores", 0), ("turn", 3), ("scores", 1), ("turn", 0), ("scores", 2), ("turn", 1),
         ("scores", 3), ("turn", 2))

PE_SLOT = dict(y=3, turn_u=12, logits=13, turn_c=15)
ACT_SLOT = dict(turn_u=12, weigh=13, turn_c=15)
DVE_MID = dict(residual=4, norm1=6, norm2=8, squares=9, unit=11, keep=14, combine=15)
DVE_END = dict(stats1=4, stats2=6, shift=8, colmax=14)
POOL_SLOT = dict(bias=1, root1=4, root2=6, root3=9)



def seq_layer(nc, x, xT, wqk, wv, bqk, bv, wpre, wpost, imask, wout, bout, gamma, beta, mu, scale,
              w1, b1, w2, b2, cos_t, sin_t, ident_d, out):
    ctx = ExitStack()
    with ctx:
        def sb(name, shape, dt=F32):
            return ctx.enter_context(nc.sbuf_tensor(name, shape, dt))

        def sem(name):
            return ctx.enter_context(nc.semaphore(name))

        d_x1 = nc.dram_tensor("d_x1", (B, NIT, P, DIM), F32).ap()
        d_xn = nc.dram_tensor("d_xn", (B, NIT, P, DIM), F32).ap()
        d_lg = nc.dram_tensor("d_lg", (B, NIT, P, ES), F32).ap()
        d_ct = nc.dram_tensor("d_ct", (B, NIT, P, KT, P), F32).ap()

        big = sb("big", [P, JT * H * GI])
        PT = big[:, :].bitcast(F16).rearrange("p (j g s i) -> p j g s i", j=JT, g=H, s=2)
        KH = sb("KH", [P, KT, N], F32R)
        KL = sb("KL", [P, KT, N], F32R)
        V = sb("V", [P, JT, H, 2, HD], F16)
        Q = sb("Q", [P, KT, N])
        AH = sb("AH", [P, TG, KT, P], F32R)
        AL = sb("AL", [P, TG, KT, P], F32R)
        at = sb("at", [P, KT, P])
        pr = sb("pr", [P, 2, N])
        ph = sb("ph", [P, 2, N], F16)
        pl = sb("pl", [P, 2, N], F16)
        rh = sb("rh", [P, P], F16)
        rl = sb("rl", [P, P], F16)
        rt = sb("rt", [P, P])
        wpre_s = sb("wpre_s", [P, H])
        wpre_q = sb("wpre_q", [P, H])
        wpost_s = sb("wpost_s", [P, H])
        imask_s = sb("imask_s", [P, QI])
        bqk_s = sb("bqk_s", [P, 4])
        bv_s = sb("bv_s", [P, DIM])
        wout_s = sb("wout_s", [P, GQ, DIM])
        bout_s = sb("bout_s", [P, DIM])
        gamma_s = sb("gamma_s", [P, DIM])
        beta_s = sb("beta_s", [P, DIM])
        scale_s = sb("scale_s", [P, 1])
        mu_s = sb("mu_s", [P, KT, ES])
        ident = sb("ident", [P, P])
        ones = sb("ones", [P, P])
        mx = sb("mx", [P, NC])
        nmax = sb("nmax", [P, 1])
        sums = sb("sums", [P, NC])
        tot = sb("tot", [P, 1])
        rec = sb("rec", [P, 1])
        rs = sb("rs", [P, 1])
        ot = sb("ot", [P, GQ, P])
        xr = sb("xr", [P, DIM])
        xb = sb("xb", [P, DIM])
        t1 = sb("t1", [P, DIM])
        x1 = sb("x1", [P, DIM])
        xn = sb("xn", [P, DIM])
        xu = sb("xu", [P, DIM])
        xuT = sb("xuT", [P, KT, P])
        lg = sb("lg", [P, ES])
        ew = sb("ew", [P, ES])
        cT = sb("cT", [P, KT, P])
        colmax = sb("colmax", [P, ES])
        st = sb("st", [P, 6])
        mv = sb("mv", [P, 2])
        va = sb("va", [P, JT])
        ya = sb("ya", [P, JT])
        za = sb("za", [P, JT])
        ia = sb("ia", [P, JT], I32)
        nrm = sb("nrm", [P, 1])
        es_ = sb("es_", [P, 1])
        er = sb("er", [P, 1])
        mv2 = sb("mv2", [P, JT, 2])
        sts = sb("sts", [P, JT, 6])
        tt = sb("tt", [P, 1])

        o = 0

        def part(n):
            nonlocal o
            v = big[:, o:o + n]
            o += n
            return v

        cos_s, sin_s = pr[:, 0, :], pr[:, 1, :]
        phf = ph[:, :, :].rearrange("p a n -> p (a n)").bitcast(F32)
        plf = pl[:, :, :].rearrange("p a n -> p (a n)").bitcast(F32)
        wqk_s = plf[:, 0:KT * 4 * P].rearrange("p (k f) -> p k f", k=KT)
        wv_s = plf[:, KT * 4 * P:KT * (4 * P + DIM)].rearrange("p (k f) -> p k f", k=KT)
        xT_s = [phf[:, i * KT * CW:(i + 1) * KT * CW].rearrange("p (k n) -> p k n", k=KT) for i in range(2)]
        raw = [part(4 * CW).rearrange("p (o n) -> p o n", o=4) for _ in range(2)]
        ta, tb, tc, td, kr0, kr1 = [part(CW) for _ in range(6)]
        vb = part(2 * DIM).rearrange("p (j g d) -> p j g d", j=2, g=H)
        o = 0
        XN = part(JT * (DIM + 1)).rearrange("p (r d) -> p r d", r=JT)
        LG = part(JT * ES).rearrange("p (r e) -> p r e", r=JT)
        CT = part(JT * ES).rearrange("p (r e) -> p r e", r=JT)
        MB = part(ES)
        si = part(KT * DIM).rearrange("p (k d) -> p k d", k=KT)
        siT = part(KT * ES).rearrange("p (k e) -> p k e", k=KT)
        dg = part(KT * P).rearrange("p (k e) -> p k e", k=KT)
        SO = part(KT * DIM).rearrange("p (k d) -> p k d", k=KT)
        HB = part(EP * S).rearrange("p (a s) -> p a s", a=EP)
        HDg = part(EP * 2 * S).rearrange("p (a s) -> p a s", a=EP)
        Qf = Q[:, :, :].rearrange("p k n -> p (k n)")
        w1_s = Qf[:, 0:KT * E * HID].rearrange("p (k e h) -> p k e h", k=KT, e=E)
        w2_s = Qf[:, KT * E * HID:KT * E * HID + EP * DIM].rearrange("p (a d) -> p a d", a=EP)
        b2_s = part(KT * DIM).rearrange("p (k d) -> p k d", k=KT)
        b1_s, cm, rslot = part(EP), part(KT), part(KT)
        X1 = V[:, :, :, :, :].rearrange("p j g s d -> p j (g s d)").bitcast(F32)

        psS = ctx.enter_context(nc.psum_tensor("psS", [P, NC + 1, CW], F32))
        psP = ctx.enter_context(nc.psum_tensor("psP", [P, 2, CW], F32))
        psO = ctx.enter_context(nc.psum_tensor("psO", [P, CW], F32))
        psM = psO

        def bank(t, c):
            return NC if c == 0 and t % 2 else c

        s_const = sem("s_const")
        s_setup = sem("s_setup")
        s_carry = sem("s_carry")
        s_gone = sem("s_gone")
        s_w = sem("s_w")
        s_xT = [sem("s_xT0"), sem("s_xT1")]
        s_qk = sem("s_qk")
        s_raw = sem("s_raw")
        s_v = sem("s_v")
        s_vc = sem("s_vc")
        s_vh = sem("s_vh")
        s_vl = sem("s_vl")
        s_rk = sem("s_rk")
        s_kh = sem("s_kh")
        s_rq = sem("s_rq")
        s_A = sem("s_A")
        s_S = sem("s_S")
        s_mx = sem("s_mx")
        s_exp = sem("s_exp")
        s_rs = sem("s_rs")
        s_pn = sem("s_pn")
        s_ph = sem("s_ph")
        s_pl = sem("s_pl")
        s_plg = sem("s_plg")
        s_D = sem("s_D")
        s_mh = sem("s_mh")
        s_ml = sem("s_ml")
        s_F = sem("s_F")
        s_oc = sem("s_oc")
        s_xr = sem("s_xr")
        s_xb = sem("s_xb")
        s_y = sem("s_y")
        s_dv = sem("s_dv")
        s_nw = sem("s_nw")
        s_t1 = sem("s_t1")
        s_seed = sem("s_seed")
        s_root = sem("s_root")
        s_x1 = sem("s_x1")
        s_xn = sem("s_xn")
        s_xu = sem("s_xu")
        s_xuT = sem("s_xuT")
        s_xuTc = sem("s_xuTc")
        s_L = sem("s_L")
        s_Lc = sem("s_Lc")
        s_nrm = sem("s_nrm")
        s_E = sem("s_E")
        s_C = sem("s_C")
        s_CT = sem("s_CT")
        s_CTc = sem("s_CTc")
        s_st = sem("s_st")
        s_ld = sem("s_ld")
        s_ldc = sem("s_ldc")
        s_mp = sem("s_mp")
        s_md = sem("s_md")
        s_ma = sem("s_ma")
        s_out = sem("s_out")

        FROM_ONE = [s_A, s_rs, s_pl, s_plg, s_D, s_F, s_y, s_mx, s_exp, s_ph,
                    s_mh, s_ml, s_oc, s_CTc, s_t1, s_xb, s_st, s_nw]

        block = ctx.enter_context(nc.Block())

        CONSTS = [(wpre_s[:, :], wpre), (wpost_s[:, :], wpost), (imask_s[:, :], imask), (bqk_s[:, :], bqk),
                  (bv_s[:, :], bv), (wout_s[:, :, :], wout), (bout_s[:, :], bout),
                  (gamma_s[:, :], gamma), (beta_s[:, :], beta), (scale_s[:, :], scale),
                  (mu_s[:, :, :], mu), (ident[:, :], ident_d)]

        def apart(e):
            e.sem_inc(s_carry, 1)

        def barrier(e, k):
            e.drain().then_inc(s_gone, 1)
            e.wait_ge(s_gone, 5 * k)
            apart(e)

        MEET = 3

        MP_MAXT, MP_MB, MP_SLOTS = 1, 2, 3
        MP_SIT, MP_H, MP_SO = 4, 5, 6
        MP = 6 + JT
        MD_CM, MD_DG = 1, 2
        MD_MB = 3
        MD_SUB = 4
        MD_REC, MD_SI, MD_SIT, MD_HB, MD_HZ, MD_SO = 9, 10, 11, 12, 13, 14
        MD_ROW = MD_SO
        MD_OUT = MD_ROW + 2 * JT + 1 + 3 + 4 * NEWTON
        MD = MD_OUT + 4
        MA = 6

        @block.sync
        def _(sp):
            for dst, src in CONSTS:
                sp.dma_start(dst, src).then_inc(s_const, 16)

            def tables():
                sp.dma_start(wqk_s, wqk).then_inc(s_w, 16)
                sp.dma_start(wv_s, wv).then_inc(s_w, 16)
                sp.dma_start(cos_s, cos_t).then_inc(s_w, 16)
                sp.dma_start(sin_s, sin_t).then_inc(s_w, 16)

            tables()
            barrier(sp, 1)
            with sp.Fori(0, B) as b:
                for c in range(NC):
                    if c >= 2:
                        sp.wait_ge(s_v, b * (NC * 2) + 2 * (c - 1))
                    sp.dma_start(xT_s[c % 2], xT[b][:, :, c * CW:(c + 1) * CW]).then_inc(s_xT[c % 2], 16)
                barrier(sp, b * MEET + 2)

                def row_load(r):
                    R = b * NIT + r
                    sp.wait_ge(s_xb, R + 1)
                    sp.dma_start(xr[:, :], x[b][r]).then_inc(s_xr, 16)

                def row_stores(r):
                    R = b * NIT + r
                    sp.wait_ge(s_x1, R + 1)
                    sp.dma_start(d_x1[b][r], x1[:, :]).then_inc(s_st, 16)
                    sp.wait_ge(s_xn, R + 1)
                    sp.dma_start(d_xn[b][r], xn[:, :]).then_inc(s_st, 16)
                    sp.wait_ge(s_Lc, R + 1)
                    sp.dma_start(d_lg[b][r], lg[:, :]).then_inc(s_st, 16)
                    sp.wait_ge(s_CTc, R + 1 + 1)
                    sp.dma_start(d_ct[b][r], cT[:, :, :]).then_inc(s_st, 16)

                def moe_rows(r0, r1):
                    sp.dma_start(LG[:, r0:r1, :], d_lg[b][r0:r1].rearrange("r p e -> p r e")).then_inc(s_ld, 16)
                    sp.dma_start(XN[:, r0:r1, 0:DIM], d_xn[b][r0:r1].rearrange("r p d -> p r d")).then_inc(s_ld, 16)
                    sp.dma_start(CT[:, r0:r1, :], d_ct[b][r0:r1].rearrange("r p k n -> p r (k n)"))\
                      .then_inc(s_ldc, 16)
                    sp.dma_start(X1[:, r0:r1, :], d_x1[b][r0:r1].rearrange("r p d -> p r d")).then_inc(s_ldc, 16)

                with sp.Fori(0, NIT - 1) as r:
                    row_load(r)
                    row_stores(r)
                row_load(NIT - 1)
                tiles = (b + 1) * (NIT * TI)
                sp.wait_ge(s_F, (b + 1) * (2 * NIT) + 1)
                sp.wait_ge(s_A, tiles * 3 + 1)
                sp.wait_ge(s_st, (b + 1) * (64 * NIT) - 64 + 1)
                moe_rows(0, NIT - 1)
                sp.dma_start(w1_s, w1).then_inc(s_ld, 16)
                sp.dma_start(w2_s, w2).then_inc(s_ld, 16)
                sp.dma_start(b1_s, b1).then_inc(s_ld, 16)
                sp.dma_start(b2_s, b2).then_inc(s_ld, 16)
                row_stores(NIT - 1)
                sp.wait_ge(s_st, (b + 1) * (64 * NIT) + 1)
                apart(sp)
                moe_rows(NIT - 1, NIT)
                tables()
                barrier(sp, b * MEET + 3)
                for q in range(4):
                    sp.wait_ge(s_md, b * MD + MD_OUT + q + 1)
                    sp.dma_start(out[b][4 * q:4 * q + 4].rearrange("r p d -> p r d"),
                                 X1[:, 4 * q:4 * q + 4, :]).then_inc(s_out, 16)
                sp.wait_ge(s_out, (b + 1) * 64)
                apart(sp)
                barrier(sp, b * MEET + 4)
            sp.wait_ge(s_w, (B + 1) * 64)

        @block.gpsimd
        def _(g):
            for s_ in FROM_ONE:
                g.sem_inc(s_, 1)
            g.memset(ones[:, :], 1.0).then_inc(s_setup, 1)
            barrier(g, 1)
            with g.Fori(0, B) as b:
                for c in range(NC):
                    n = slice(c * CW, (c + 1) * CW)
                    g.wait_ge(s_w, b * 64 + 64)
                    g.wait_ge(s_raw, b * (4 * NC) + 4 * c + 2)
                    q0, q1 = raw[c % 2][:, 0, :], raw[c % 2][:, 1, :]
                    base = b * (6 * NC) + 6 * c
                    if c >= 1:
                        g.wait_ge(s_rq, base)
                    g.tensor_tensor(tc, q0, cos_s[:, n], ALU.mult).then_inc(s_rq, 1)
                    g.tensor_tensor(td, q1, sin_s[:, n], ALU.mult).then_inc(s_rq, 1)
                    g.wait_ge(s_rq, base + 2)
                    g.tensor_tensor(Q[:, 0, n], tc, td, ALU.subtract).then_inc(s_rq, 1)
                    g.wait_ge(s_rq, base + 3)
                    g.tensor_tensor(tc, q0, sin_s[:, n], ALU.mult).then_inc(s_rq, 1)
                    g.tensor_tensor(td, q1, cos_s[:, n], ALU.mult).then_inc(s_rq, 1)
                    g.wait_ge(s_rq, base + 5)
                    g.tensor_tensor(Q[:, 1, n], tc, td, ALU.add).then_inc(s_rq, 1)
                barrier(g, b * MEET + 2)

                def premix(it, t, fresh):
                    T = (b * NIT + it) * TI + t
                    if not fresh:
                        g.wait_ge(s_S, T * NC - (TG - 1) * NC)
                    g.wait_ge(s_A, T * 3 + 1)
                    k = t % TG
                    i0 = it * (TI * QI) + t * QI
                    v = at[:, :, :].rearrange("p k (g i) -> p k g i", g=H)
                    g.tensor_tensor(v, Q[:, :, bass.ds(i0, QI)].unsqueeze(2).broadcast_to([P, KT, H, QI]),
                                    wpre_q[:, :].unsqueeze(1).unsqueeze(3).broadcast_to([P, KT, H, QI]),
                                    ALU.mult).then_inc(s_A, 1)
                    g.wait_ge(s_A, T * 3 + 1 + 1)
                    apart(g)
                    g.tensor_copy(AH[:, k, :, :], at[:, :, :]).then_inc(s_A, 1)
                    g.wait_ge(s_A, T * 3 + 2 + 1)
                    g.tensor_tensor(AL[:, k, :, :], at[:, :, :], AH[:, k, :, :].bitcast(F32),
                                    ALU.subtract).then_inc(s_A, 1)

                def add_bias(r):
                    R = b * NIT + r
                    g.wait_ge(s_xr, R * 16 + 16)
                    g.wait_ge(s_t1, R + 1)
                    g.tensor_tensor(xb[:, :], xr[:, :], bout_s[:, :], ALU.add).then_inc(s_xb, 1)

                def newton(r, k):
                    R = b * NIT + r
                    NW = 4 * NEWTON * 3
                    g.wait_ge(s_seed, R * 3 + k + 1)
                    v, y, z = va[:, 0:1], ya[:, 0:1], za[:, 0:1]
                    n = 4 * NEWTON * k
                    for m in range(NEWTON):
                        ops = [lambda: g.tensor_tensor(z, y, y, ALU.mult),
                               lambda: g.tensor_tensor(z, z, v, ALU.mult),
                               lambda: g.tensor_scalar(z, z, -0.5, 1.5, ALU.mult, ALU.add)]
                        for op in ops:
                            g.wait_ge(s_nw, R * NW + n + 1)
                            apart(g)
                            op().then_inc(s_nw, 1)
                            n += 1
                        g.wait_ge(s_nw, R * NW + n + 1)
                        g.tensor_tensor(y, y, z, ALU.mult).then_inc(s_nw, 1)
                        n += 1
                    g.wait_ge(s_nw, R * NW + n + 1)
                    apart(g)
                    if k < 2:
                        g.tensor_copy(z, y).then_inc(s_root, 1)
                    else:
                        g.tensor_tensor(z, y, scale_s[:, :], ALU.mult).then_inc(s_root, 1)

                WORK = {POOL_SLOT["bias"]: add_bias, POOL_SLOT["root1"]: lambda r: newton(r, 0),
                        POOL_SLOT["root2"]: lambda r: newton(r, 1),
                        POOL_SLOT["root3"]: lambda r: newton(r, 2)}

                def low(T, t, early):
                    g.wait_ge(s_ph, T * 3 + 3 + 1)
                    if not early:
                        g.wait_ge(s_D, (T - 1) * NC + 1)
                    g.tensor_tensor(pl[:, t % 2, NL:N], pr[:, t % 2, NL:N], ph[:, t % 2, NL:N],
                                    ALU.subtract).then_inc(s_plg, 1)

                for t in range(TG):
                    premix(0, t, True)
                for t in range(TI):
                    premix(0, t + TG, False)
                    low(b * (NIT * TI) + t, t, t < 2)
                with g.Fori(1, NIT - 1) as it:
                    for t in range(TI):
                        premix(it, t + TG, False)
                        low((b * NIT + it) * TI + t, t, False)
                        if t in WORK:
                            WORK[t](it - 1)
                for t in range(TI):
                    if t + TG < TI:
                        premix(NIT - 1, t + TG, False)
                    low((b * NIT + NIT - 1) * TI + t, t, False)
                    if t in WORK:
                        WORK[t](NIT - 2)
                for t in sorted(WORK):
                    WORK[t](NIT - 1)
                barrier(g, b * MEET + 3)
                barrier(g, b * MEET + 4)

        @block.scalar
        def _(a):
            barrier(a, 1)
            with a.Fori(0, B) as b:
                for c in range(NC):
                    for f in range(4):
                        a.wait_ge(s_qk, b * (4 * NC) + 4 * c + f + 1)
                        if c >= 2:
                            a.wait_ge(s_rq, b * (6 * NC) + 6 * (c - 1))
                            a.wait_ge(s_rk, b * (8 * NC) + 8 * (c - 1))
                        a.activation(raw[c % 2][:, f, :], psS[:, f, :], ACT.Identity,
                                     bias=bqk_s[:, f:f + 1]).then_inc(s_raw, 1)
                    for k, kr in enumerate((kr0, kr1)):
                        a.wait_ge(s_rk, b * (8 * NC) + 8 * c + 3 + 3 * k)
                        a.activation(KH[:, k, c * CW:(c + 1) * CW], kr, ACT.Copy).then_inc(s_kh, 1)
                barrier(a, b * MEET + 2)

                def exps(T, t, c, early):
                    cs = slice(c * CW, (c + 1) * CW)
                    if c == EXPS[0]:
                        a.wait_ge(s_mx, T * 5 + 5 + 1)
                        a.wait_ge(s_rs, T * 3 + 1)
                        if not early:
                            a.wait_ge(s_pl, (T - 1) * 2 + 1)
                            a.wait_ge(s_plg, T - 1 + 1)
                    a.activation(pr[:, t % 2, cs], psS[:, bank(t, c), :], ACT.Exp, bias=nmax[:, 0:1], scale=1.0,
                                 accum_out=sums[:, c:c + 1]).then_inc(s_exp, 1)

                def mixed_high(T, t, c, Gd):
                    a.wait_ge(s_D, T * NC + c + 1 + 1)
                    if t % TG == 0 and c == 0:
                        a.wait_ge(s_F, Gd + 1)
                    i0 = (t % TG) * QI
                    a.activation(PT[:, c * JC:(c + 1) * JC, :, 0, i0:i0 + QI],
                                 psP[:, c % 2, :].rearrange("p (j g i) -> p j g i", j=JC, g=H),
                                 ACT.Copy).then_inc(s_mh, 1)

                def highs(T, t, early, mixed):
                    a.wait_ge(s_rs, T * 3 + 3 + 1)
                    if not early:
                        a.wait_ge(s_D, (T - 1) * NC + 1)
                    p_, h_ = pr[:, t % 2, :], ph[:, t % 2, :]
                    a.activation(h_[:, 0:N2], p_[:, 0:N2], ACT.Copy, scale=rs[:, 0:1]).then_inc(s_ph, 1)
                    mixed(1, 0)
                    a.activation(p_[:, NL:N], p_[:, NL:N], ACT.Copy, scale=rs[:, 0:1]).then_inc(s_pn, 1)
                    a.activation(h_[:, N2:NL], p_[:, N2:NL], ACT.Copy, scale=rs[:, 0:1]).then_inc(s_ph, 1)
                    a.wait_ge(s_pn, T + 1)
                    a.activation(h_[:, NL:N], p_[:, NL:N], ACT.Copy).then_inc(s_ph, 1)

                def turn(r):
                    R = b * NIT + r
                    a.wait_ge(s_xuT, R + 1)
                    a.activation(xuT[:, :, :], psM[:, 0:DIM].rearrange("p (k n) -> p k n", k=KT),
                                 ACT.Copy).then_inc(s_xuTc, 1)

                def weigh(r):
                    R = b * NIT + r
                    a.wait_ge(s_nrm, R + 1)
                    a.activation(ew[:, :], lg[:, :], ACT.Exp, bias=nrm[:, 0:1], scale=1.0,
                                 accum_out=es_[:, 0:1]).then_inc(s_E, 1)

                def store_c(r):
                    R = b * NIT + r
                    a.wait_ge(s_CT, R + 1)
                    a.activation(cT[:, :, :], psM[:, 0:ES].rearrange("p (k n) -> p k n", k=KT),
                                 ACT.Copy).then_inc(s_CTc, 1)

                WORK = {ACT_SLOT["turn_u"]: turn, ACT_SLOT["weigh"]: weigh, ACT_SLOT["turn_c"]: store_c}

                def slot(it, t, first):
                    T = (b * NIT + it) * TI + t
                    early = first and t < 2
                    def mixed(d, c):
                        if not (first and t < d):
                            mixed_high(T - d, (t - d) % TI, c, (b * NIT + it) * 2 + (t - d) // TG)
                    exps(T, t, EXPS[0], early)
                    exps(T, t, EXPS[1], early)
                    mixed(2, 2)
                    exps(T, t, EXPS[2], early)
                    exps(T, t, EXPS[3], early)
                    mixed(2, 3)
                    highs(T, t, early, mixed)
                    mixed(1, 1)

                for t in range(TI):
                    slot(0, t, True)
                with a.Fori(1, NIT) as it:
                    for t in range(TI):
                        slot(it, t, False)
                        if t in WORK:
                            WORK[t](it - 1)
                Tl = (b * NIT + NIT) * TI
                for t, c in ((2, 2), (2, 3), (1, 0), (1, 1), (1, 2), (1, 3)):
                    mixed_high(Tl - t, TI - t, c, 0)
                for t in sorted(WORK):
                    WORK[t](NIT - 1)
                barrier(a, b * MEET + 3)

                for q in range(4):
                    a.wait_ge(s_md, b * MD + MD_SUB + q + 1)
                    v = LG[:, 4 * q:4 * q + 4, :]
                    a.activation(v, v, ACT.Exp).then_inc(s_ma, 1)
                a.wait_ge(s_md, b * MD + MD_HZ)
                for e2 in range(2):
                    rows = slice(e2 * HID, (e2 + 1) * HID)
                    a.activation(HDg[rows, :, e2 * S:(e2 + 1) * S], HB[rows, :, :], ACT.Gelu)\
                        .then_inc(s_ma, 1)
                barrier(a, b * MEET + 4)

        @block.vector
        def _(v):
            v.wait_ge(s_const, 16 * len(CONSTS))
            v.tensor_scalar(wout_s[:, :, :], wout_s[:, :, :], 1.0 / PSCALE, None, ALU.mult).then_inc(s_setup, 1)
            v.wait_ge(s_setup, 2)
            v.tensor_scalar(wpre_q[:, :], wpre_s[:, :], float(HD) ** -0.5, None, ALU.mult).then_inc(s_setup, 1)
            v.tensor_tensor(rt[:, :].rearrange("p (g i) -> p g i", g=H),
                            wpost_s[:, :].unsqueeze(2).broadcast_to([P, H, QI]),
                            imask_s[:, :].unsqueeze(1).broadcast_to([P, H, QI]), ALU.mult).then_inc(s_setup, 1)
            v.wait_ge(s_setup, 4)
            v.tensor_copy(rh[:, :], rt[:, :]).then_inc(s_setup, 1)
            v.wait_ge(s_setup, 5)
            v.tensor_tensor(rl[:, :], rt[:, :], rh[:, :], ALU.subtract).then_inc(s_setup, 1)
            sq = big[:, 0:KT * ES].rearrange("p (k e) -> p k e", k=KT)
            mv_, my, mz, mi = (big[:, 1024 + 256 * k:1280 + 256 * k] for k in range(4))
            mi = mi.bitcast(I32)
            v.tensor_tensor(sq, mu_s[:, :, :], mu_s[:, :, :], ALU.mult).then_inc(s_setup, 1)
            v.wait_ge(s_setup, 8)
            v.tensor_scalar(mv_, psM[:, 0:ES], NORM_EPS2, None, ALU.max).then_inc(s_setup, 1)
            n = 9

            def link(ins):
                nonlocal n
                ins.then_inc(s_setup, 1)
                n += 1
                v.wait_ge(s_setup, n)

            v.wait_ge(s_setup, 9)
            link(v.tensor_scalar(mi, mv_.bitcast(I32), 1, None, ALU.logical_shift_right))
            link(v.tensor_scalar(my.bitcast(I32), mi, -1.0, MAGIC, ALU.mult, ALU.add))
            for _ in range(NEWTON):
                link(v.tensor_tensor(mz, my, my, ALU.mult))
                link(v.tensor_tensor(mz, mz, mv_, ALU.mult))
                link(v.tensor_scalar(mz, mz, -0.5, 1.5, ALU.mult, ALU.add))
                link(v.tensor_tensor(my, my, mz, ALU.mult))
            link(v.tensor_tensor(mu_s[:, :, :], mu_s[:, :, :], my.unsqueeze(1).broadcast_to([P, KT, ES]), ALU.mult))
            barrier(v, 1)

            with v.Fori(0, B) as b:
                v.memset(colmax[:, :], LOW).then_inc(s_dv, 1)
                for c in range(NC):
                    n_ = slice(c * CW, (c + 1) * CW)
                    v.wait_ge(s_w, b * 64 + 64)
                    for h in range(2):
                        v.wait_ge(s_v, b * (2 * NC) + 2 * c + h + 1)
                        n_v = b * (2 * NC) + 2 * c + h
                        if 2 * c + h >= 1:
                            v.wait_ge(s_vl, n_v)
                        v.tensor_tensor(vb.rearrange("p j g d -> p j (g d)"),
                                        psP[:, h, :].rearrange("p (j d) -> p j d", j=2),
                                        bv_s[:, :].unsqueeze(1).broadcast_to([P, 2, DIM]),
                                        ALU.add).then_inc(s_vc, 1)
                        vh, vl = (V[:, JC * c + 2 * h:JC * c + 2 * h + 2, :, s_, :] for s_ in range(2))
                        v.wait_ge(s_vc, n_v + 1)
                        v.tensor_copy(vh, vb).then_inc(s_vh, 1)
                        v.wait_ge(s_vh, n_v + 1)
                        v.tensor_tensor(vl, vb, vh, ALU.subtract).then_inc(s_vl, 1)
                    v.wait_ge(s_raw, b * (4 * NC) + 4 * c + 4)
                    base = b * (8 * NC) + 8 * c
                    k0, k1 = raw[c % 2][:, 2, :], raw[c % 2][:, 3, :]
                    if c >= 1:
                        v.wait_ge(s_rk, base)
                    v.tensor_tensor(ta, k0, cos_s[:, n_], ALU.mult).then_inc(s_rk, 1)
                    v.tensor_tensor(tb, k1, sin_s[:, n_], ALU.mult).then_inc(s_rk, 1)
                    v.wait_ge(s_rk, base + 2)
                    v.tensor_tensor(kr0, ta, tb, ALU.subtract).then_inc(s_rk, 1)
                    v.wait_ge(s_rk, base + 3)
                    v.tensor_tensor(ta, k0, sin_s[:, n_], ALU.mult).then_inc(s_rk, 1)
                    v.tensor_tensor(tb, k1, cos_s[:, n_], ALU.mult).then_inc(s_rk, 1)
                    v.wait_ge(s_rk, base + 5)
                    v.tensor_tensor(kr1, ta, tb, ALU.add).then_inc(s_rk, 1)
                    for k, kr in enumerate((kr0, kr1)):
                        v.wait_ge(s_kh, b * (2 * NC) + 2 * c + k + 1)
                        v.wait_ge(s_rk, base + 6)
                        v.tensor_tensor(KL[:, k, n_], kr, KH[:, k, n_].bitcast(F32),
                                        ALU.subtract).then_inc(s_rk, 1)
                barrier(v, b * MEET + 2)

                def chunk_max(T, t, c):
                    v.wait_ge(s_S, T * NC + c + 1)
                    if c == 0:
                        v.wait_ge(s_mx, T * 5 + 1)
                    v.tensor_reduce(mx[:, c:c + 1], psS[:, bank(t, c), :], X, ALU.max).then_inc(s_mx, 1)

                def tile_max(T):
                    v.wait_ge(s_mx, T * 5 + 4 + 1)
                    v.wait_ge(s_exp, T * NC + 1)
                    v.tensor_reduce(nmax[:, 0:1], mx[:, :], X, ALU.max, negate=True).then_inc(s_mx, 1)

                def mixed_low(T, t, c):
                    v.wait_ge(s_mh, T * NC + c + 1 + 1)
                    i0 = (t % TG) * QI
                    js = slice(c * JC, (c + 1) * JC)
                    v.tensor_tensor(PT[:, js, :, 1, i0:i0 + QI],
                                    psP[:, c % 2, :].rearrange("p (j g i) -> p j g i", j=JC, g=H),
                                    PT[:, js, :, 0, i0:i0 + QI], ALU.subtract).then_inc(s_ml, 1)

                def out_copy(Gd, half, R):
                    v.wait_ge(s_F, Gd + 1 + 1)
                    v.wait_ge(s_y, R + 1)
                    v.tensor_reduce(ot[:, :, half * GI:(half + 1) * GI],
                                    psO[:, :].rearrange("p (q s i) -> p q i s", q=GQ, s=2), X,
                                    ALU.add).then_inc(s_oc, 1)

                def recip(T):
                    v.wait_ge(s_exp, T * NC + NC + 1)
                    v.wait_ge(s_ph, T * 3 + 1)
                    v.wait_ge(s_pl, T * 2 + 1)
                    v.wait_ge(s_plg, T + 1)
                    v.tensor_reduce(tot[:, 0:1], sums[:, :], X, ALU.add).then_inc(s_rs, 1)
                    v.wait_ge(s_rs, T * 3 + 1 + 1)
                    v.reciprocal(rec[:, 0:1], tot[:, 0:1]).then_inc(s_rs, 1)
                    v.wait_ge(s_rs, T * 3 + 2 + 1)
                    v.tensor_scalar(rs[:, 0:1], rec[:, 0:1], PSCALE, None, ALU.mult).then_inc(s_rs, 1)

                def low(T, t, h, early):
                    cs = (slice(0, N2), slice(N2, NL))[h]
                    v.wait_ge(s_ph, T * 3 + h + 1 + 1)
                    if h == 0:
                        v.wait_ge(s_rs, T * 3 + 3 + 1)
                        if not early:
                            v.wait_ge(s_D, (T - 1) * NC + 1)
                    v.scalar_tensor_tensor(out=pl[:, t % 2, cs], in0=pr[:, t % 2, cs], scalar=rs[:, 0:1],
                                           in1=ph[:, t % 2, cs], op0=ALU.mult, op1=ALU.subtract)\
                        .then_inc(s_pl, 1)

                DV = 15
                cnt = [0]

                def chain(R, ins):
                    ins.then_inc(s_dv, 1)
                    cnt[0] += 1
                    v.wait_ge(s_dv, R * DV + cnt[0] + b + 1)
                    apart(v)

                def seed(R, src, low, op):
                    chain(R, v.tensor_scalar(va[:, 0:1], src, low, None, op))
                    chain(R, v.tensor_scalar(ia[:, 0:1], va[:, 0:1].bitcast(I32), 1, None,
                                             ALU.logical_shift_right))
                    v.tensor_scalar(ya[:, 0:1].bitcast(I32), ia[:, 0:1], -1.0, MAGIC,
                                    ALU.mult, ALU.add).then_inc(s_seed, 1)

                def residual(r):
                    R = b * NIT + r
                    cnt[0] = 0
                    v.wait_ge(s_y, R + 1 + 1)
                    v.wait_ge(s_xb, R + 1 + 1)
                    v.tensor_tensor(t1[:, :], psM[:, 0:DIM], xb[:, :], ALU.add).then_inc(s_t1, 1)
                    v.wait_ge(s_t1, R + 1 + 1)
                    chain(R, v.bn_stats(st[:, :], t1[:, :]))

                def stats(r):
                    R = b * NIT + r
                    chain(R, v.bn_aggr(mv[:, :], st[:, :]))
                    seed(R, mv[:, 1:2], LN_EPS, ALU.add)

                def norm1(r):
                    R = b * NIT + r
                    v.wait_ge(s_root, R * 3 + 1)
                    v.wait_ge(s_st, R * 64 + 1)
                    v.tensor_scalar(x1[:, :], t1[:, :], mv[:, 0:1], za[:, 0:1],
                                    ALU.subtract, ALU.mult).then_inc(s_x1, 1)
                    v.wait_ge(s_x1, R + 1)
                    chain(R, v.bn_stats(st[:, :], x1[:, :]))

                def norm2(r):
                    R = b * NIT + r
                    v.wait_ge(s_root, R * 3 + 2)
                    chain(R, v.tensor_scalar(t1[:, :], x1[:, :], mv[:, 0:1], za[:, 0:1],
                                             ALU.subtract, ALU.mult))
                    chain(R, v.tensor_tensor(t1[:, :], t1[:, :], gamma_s[:, :], ALU.mult))

                def shift(r):
                    R = b * NIT + r
                    v.tensor_tensor(xn[:, :], t1[:, :], beta_s[:, :], ALU.add).then_inc(s_xn, 1)

                def squares(r):
                    R = b * NIT + r
                    v.wait_ge(s_xn, R + 1)
                    chain(R, v.tensor_tensor_reduce(out=t1[:, :], in0=xn[:, :], in1=xn[:, :], scale=1.0,
                                                    scalar=0.0, op0=ALU.mult, op1=ALU.add,
                                                    accum_out=tt[:, 0:1]))
                    seed(R, tt[:, 0:1], NORM_EPS2, ALU.max)

                def unit(r):
                    R = b * NIT + r
                    v.wait_ge(s_root, R * 3 + 3)
                    v.tensor_scalar(xu[:, :], xn[:, :], za[:, 0:1], None, ALU.mult).then_inc(s_xu, 1)

                def keep(r):
                    R = b * NIT + r
                    v.wait_ge(s_L, R + 1)
                    v.tensor_copy(lg[:, :], psM[:, 0:ES]).then_inc(s_Lc, 1)
                    v.wait_ge(s_Lc, R + 1)
                    v.tensor_reduce(nrm[:, 0:1], lg[:, :], X, ALU.max, negate=True).then_inc(s_nrm, 1)

                def column(r):
                    R = b * NIT + r
                    chain(R, v.tensor_tensor(colmax[:, :], colmax[:, :], lg[:, :], ALU.max))

                def combine(r):
                    R = b * NIT + r
                    v.wait_ge(s_E, R + 1)
                    chain(R, v.reciprocal(er[:, 0:1], es_[:, 0:1]))
                    v.tensor_scalar(ew[:, :], ew[:, :], er[:, 0:1], None, ALU.mult).then_inc(s_C, 1)

                MID = {DVE_MID["residual"]: residual, DVE_MID["norm1"]: norm1, DVE_MID["norm2"]: norm2,
                       DVE_MID["squares"]: squares, DVE_MID["unit"]: unit, DVE_MID["keep"]: keep,
                       DVE_MID["combine"]: combine}
                END = {DVE_END["stats1"]: stats, DVE_END["stats2"]: stats, DVE_END["shift"]: shift,
                       DVE_END["colmax"]: column}

                def slot(it, t, first, work):
                    T = (b * NIT + it) * TI + t
                    Gp = (b * NIT + it) * 2 + (t - 3) // TG
                    def mixed(d, c):
                        if not (first and t < d):
                            mixed_low(T - d, (t - d) % TI, c)
                    mixed(3, 2)
                    chunk_max(T, t, 0)
                    if not (first and t < 1):
                        recip(T - 1)
                    mixed(3, 3)
                    chunk_max(T, t, 1)
                    if work is not None and t in MID:
                        MID[t](work)
                    chunk_max(T, t, 2)
                    mixed(2, 0)
                    if work is not None and t in END:
                        END[t](work)
                    chunk_max(T, t, 3)
                    tile_max(T)
                    mixed(2, 1)
                    if not (first and t < 1):
                        low(T - 1, (t - 1) % TI, 0, first and t < 3)
                        low(T - 1, (t - 1) % TI, 1, first and t < 3)
                    if (t - 3) % TG == TG - 1 and not (first and t < 3):
                        out_copy(Gp, (t - 3) % TI // TG, b * NIT + it - (1 if t < 3 else 0))

                for t in range(TI):
                    slot(0, t, True, None)
                with v.Fori(1, NIT - 1) as it:
                    for t in range(TI):
                        slot(it, t, False, it - 1)
                for t in range(TI):
                    slot(NIT - 1, t, False, NIT - 2)
                Tl = (b * NIT + NIT) * TI
                for c in (2, 3):
                    mixed_low(Tl - 3, TI - 3, c)
                recip(Tl - 1)
                low(Tl - 1, TI - 1, 0, False)
                low(Tl - 1, TI - 1, 1, False)
                for t in (2, 1):
                    for c in range(NC):
                        mixed_low(Tl - t, TI - t, c)
                out_copy((b + 1) * (NIT * 2) - 1, 1, b * NIT + NIT - 1)
                for t in range(TI):
                    for steps in (MID, END):
                        if t in steps:
                            steps[t](NIT - 1)
                assert cnt[0] == DV, cnt
                barrier(v, b * MEET + 3)

                m0 = b * MD
                v.wait_ge(s_mp, b * MP + MP_MAXT)
                v.tensor_reduce(cm, psM[:, 0:ES].rearrange("p (k n) -> p k n", k=KT), X, ALU.max).then_inc(s_md, 1)
                v.wait_ge(s_md, m0 + MD_CM)
                v.tensor_tensor(dg, ident[:, :].unsqueeze(1).broadcast_to([P, KT, P]),
                                cm.unsqueeze(2).broadcast_to([P, KT, P]), ALU.mult).then_inc(s_md, 1)
                v.wait_ge(s_mp, b * MP + MP_MB)
                v.tensor_copy(MB, psM[:, 0:ES]).then_inc(s_md, 1)
                v.wait_ge(s_md, m0 + MD_MB)
                v.wait_ge(s_ld, b * 128 + 128)
                for q in range(4):
                    w = LG[:, 4 * q:4 * q + 4, :]
                    if q == 0:
                        v.memset(XN[:, :, DIM:DIM + 1], 1.0).then_inc(s_md, 1)
                    v.tensor_tensor(w, w, MB.unsqueeze(1).broadcast_to([P, 4, ES]), ALU.subtract).then_inc(s_md, 1)
                v.wait_ge(s_mp, b * MP + MP_SLOTS)
                v.reciprocal(rslot, psS[:, 0:2, DIM:DIM + 1].rearrange("p k a -> p (k a)")).then_inc(s_md, 1)
                v.wait_ge(s_md, m0 + MD_REC)
                v.tensor_tensor(si, psS[:, 0:2, 0:DIM], rslot.unsqueeze(2).broadcast_to([P, KT, DIM]),
                                ALU.mult).then_inc(s_md, 1)
                v.wait_ge(s_mp, b * MP + MP_SIT)
                v.tensor_copy(siT, psS[:, 2, :].rearrange("p (k e) -> p k e", k=KT)).then_inc(s_md, 1)
                v.wait_ge(s_mp, b * MP + MP_H)
                v.tensor_tensor(HB, psS[:, 3, 0:EP * S].rearrange("p (a s) -> p a s", a=EP),
                                b1_s.unsqueeze(2).broadcast_to([P, EP, S]), ALU.add).then_inc(s_md, 1)
                v.memset(HDg, 0.0).then_inc(s_md, 1)
                v.wait_ge(s_mp, b * MP + MP_SO)
                v.tensor_tensor(SO, psP[:, :, 0:DIM], b2_s, ALU.add).then_inc(s_md, 1)
                v.wait_ge(s_ldc, b * 64 + 64)
                for r in range(JT):
                    v.wait_ge(s_mp, b * MP + MP_SO + r + 1)
                    v.tensor_tensor(X1[:, r, :], psS[:, r % 4, 0:DIM], X1[:, r, :], ALU.add).then_inc(s_md, 1)
                    v.wait_ge(s_md, m0 + MD_ROW + 2 * r + 1)
                    v.bn_stats(sts[:, r, :], X1[:, r, :]).then_inc(s_md, 1)
                n = MD_ROW + 2 * JT
                v.wait_ge(s_md, m0 + n)
                apart(v)
                for r in range(JT):
                    last = v.bn_aggr(mv2[:, r, :], sts[:, r, :])
                last.then_inc(s_md, 1)
                n += 1
                v.wait_ge(s_md, m0 + n)
                apart(v)

                def step(ins):
                    nonlocal n
                    ins.then_inc(s_md, 1)
                    n += 1
                    v.wait_ge(s_md, m0 + n)

                step(v.tensor_scalar(va[:, :], mv2[:, :, 1], LN_EPS, None, ALU.add))
                step(v.tensor_scalar(ia[:, :], va[:, :].bitcast(I32), 1, None, ALU.logical_shift_right))
                step(v.tensor_scalar(ya[:, :].bitcast(I32), ia[:, :], -1.0, MAGIC, ALU.mult, ALU.add))
                for _ in range(NEWTON):
                    step(v.tensor_tensor(za[:, :], ya[:, :], ya[:, :], ALU.mult))
                    step(v.tensor_tensor(za[:, :], za[:, :], va[:, :], ALU.mult))
                    step(v.tensor_scalar(za[:, :], za[:, :], -0.5, 1.5, ALU.mult, ALU.add))
                    step(v.tensor_tensor(ya[:, :], ya[:, :], za[:, :], ALU.mult))
                assert n == MD_OUT, (n, MD_OUT)
                for r in range(JT):
                    done = v.tensor_scalar(X1[:, r, :], X1[:, r, :], mv2[:, r, 0:1], ya[:, r:r + 1],
                                           ALU.subtract, ALU.mult)
                    if r % 4 == 3:
                        done.then_inc(s_md, 1)
                barrier(v, b * MEET + 4)

        @block.tensor
        def _(pe):
            pe.wait_ge(s_setup, 7)
            for k in range(KT):
                mm = pe.matmul(psM[:, 0:ES], ones[:, :], big[:, k * ES:(k + 1) * ES], start=k == 0, stop=k == KT - 1)
            mm.then_inc(s_setup, 1)
            barrier(pe, 1)
            with pe.Fori(0, B) as b:
                pe.wait_ge(s_w, b * 64 + 64)
                for c in range(NC):
                    xc = xT_s[c % 2]
                    pe.wait_ge(s_xT[c % 2], b * (8 * NC) + 16 * (c // 2) + 16)
                    for f in range(4):
                        if c >= 1:
                            pe.wait_ge(s_raw, b * (4 * NC) + 4 * (c - 1) + f + 1)
                        for k in range(KT):
                            mm = pe.matmul(psS[:, f, :], wqk_s[:, k, f * P:(f + 1) * P], xc[:, k, :],
                                           start=k == 0, stop=k == KT - 1)
                        mm.then_inc(s_qk, 1)
                    for h in range(2):
                        if c >= 1:
                            pe.wait_ge(s_vc, b * (2 * NC) + 2 * (c - 1) + h + 1)
                        for j in range(2):
                            for k in range(KT):
                                j0 = (2 * h + j) * P
                                mm = pe.matmul(psP[:, h, j * DIM:(j + 1) * DIM], xc[:, k, j0:j0 + P],
                                               wv_s[:, k, :], start=k == 0, stop=k == KT - 1)
                        mm.then_inc(s_v, 1)
                barrier(pe, b * MEET + 2)

                def scores(T, t, c, fresh):
                    k8 = t % TG
                    if c == 0:
                        pe.wait_ge(s_A, T * 3 + 3 + 1)
                    if not fresh:
                        last = 0 if c == 0 else EXPS.index(c) + 1
                        pe.wait_ge(s_exp, (T - 1) * NC + last + 1)
                    n = 0
                    for A_, K_ in ((AH, KH), (AL, KH), (AH, KL)):
                        for k in range(KT):
                            mm = pe.matmul(psS[:, bank(t, c), :], A_[:, k8, k, :], K_[:, k, c * CW:(c + 1) * CW],
                                           start=n == 0, stop=n == 5)
                            n += 1
                    mm.then_inc(s_S, 1)

                def turn(T, t, c, fresh=False):
                    if c == 0:
                        pe.wait_ge(s_pl, T * 2 + 2 + 1)
                    if c == LC:
                        pe.wait_ge(s_plg, T + 1 + 1)
                    if not fresh:
                        pe.wait_ge(s_ml, T * NC + c - 2 + 1 + 1)
                    for j in range(JC):
                        cs = slice((c * JC + j) * P, (c * JC + j + 1) * P)
                        o_ = psP[:, c % 2, j * P:(j + 1) * P]
                        pe.matmul(o_, ph[:, t % 2, cs], rh[:, :], start=True, stop=False)
                        pe.matmul(o_, ph[:, t % 2, cs], rl[:, :], start=False, stop=False)
                        mm = pe.matmul(o_, pl[:, t % 2, cs], rh[:, :], start=False, stop=True)
                    mm.then_inc(s_D, 1)

                def output(Tn, Gd):
                    pe.wait_ge(s_oc, Gd + 1)
                    for c in range(NC):
                        pe.wait_ge(s_ml, Tn * NC - NC + c + 1 + 1)
                        for j in range(c * JC, (c + 1) * JC):
                            for q in range(GQ):
                                for w in range(4):
                                    g_ = 4 * q + w
                                    mm = pe.matmul(psO[32 * w:32 * w + 32, q * P:(q + 1) * P],
                                                   V[:, j, g_, :, :], PT[:, j, g_, :, :],
                                                   start=j == 0 and q == 0, stop=j == JT - 1,
                                                   skip_group_check=True, tile_position=(0, 32 * w))
                    mm.then_inc(s_F, 1)

                def y(r):
                    R = b * NIT + r
                    pe.wait_ge(s_oc, R * 2 + 2 + 1)
                    pe.wait_ge(s_CTc, R + 1)
                    for q in range(GQ):
                        mm = pe.matmul(psM[:, 0:DIM], ot[:, q, :], wout_s[:, q, :], start=q == 0, stop=q == GQ - 1)
                    mm.then_inc(s_y, 1)

                def turn_u(r, groups=3):
                    R = b * NIT + r
                    pe.wait_ge(s_oc, R * 2 + groups + 1)
                    pe.wait_ge(s_xu, R + 1)
                    for k in range(KT):
                        mm = pe.transpose(psM[:, k * P:(k + 1) * P], xu[:, k * P:(k + 1) * P], ident[:, :])
                    mm.then_inc(s_xuT, 1)

                def logits(r):
                    R = b * NIT + r
                    pe.wait_ge(s_xuTc, R + 1)
                    for k in range(KT):
                        mm = pe.matmul(psM[:, 0:ES], xuT[:, k, :], mu_s[:, k, :], start=k == 0, stop=k == KT - 1)
                    mm.then_inc(s_L, 1)

                def turn_c(r):
                    R = b * NIT + r
                    pe.wait_ge(s_C, R + 1)
                    for k in range(KT):
                        mm = pe.transpose(psM[:, k * P:(k + 1) * P], ew[:, k * P:(k + 1) * P], ident[:, :])
                    mm.then_inc(s_CT, 1)

                WORK = {PE_SLOT["y"]: y, PE_SLOT["turn_u"]: turn_u, PE_SLOT["logits"]: logits,
                        PE_SLOT["turn_c"]: turn_c}

                def slot(it, t, first):
                    T = (b * NIT + it) * TI + t
                    G = (b * NIT + it) * 2
                    for step, c in ORDER:
                        if step == "scores":
                            scores(T, t, c, first and t < (2 if c == 0 else 1))
                        elif not (first and t < LAG[c]):
                            turn(T - LAG[c], t - LAG[c], c, first and t == 2 and c < 2)
                        if (step, c) == ("scores", 1) and (t - 2) % TG == 0 and not (first and t < 3):
                            if t == 2:
                                pe.wait_ge(s_CTc, b * NIT + it - 1 + 1)
                            else:
                                pe.wait_ge(s_t1, b * NIT + it + 1)
                            output(T - 2, G + (t - 3) // TG)

                for t in range(TI):
                    slot(0, t, True)
                with pe.Fori(1, NIT) as it:
                    for t in range(TI):
                        slot(it, t, False)
                        if t in WORK:
                            WORK[t](it - 1)
                Tl = (b * NIT + NIT) * TI
                turn(Tl - 3, TI - 3, NC - 1)
                for t in (2, 1):
                    for c in range(NC):
                        turn(Tl - t, TI - t, c)
                pe.wait_ge(s_CTc, (b + 1) * NIT - 1 + 1)
                output(Tl, (b + 1) * (NIT * 2) - 1)
                for work in (y, lambda r: turn_u(r, 2), logits, turn_c):
                    work(NIT - 1)
                barrier(pe, b * MEET + 3)

                m0 = b * MP
                for k in range(KT):
                    mm = pe.transpose(psM[:, k * P:(k + 1) * P], colmax[:, k * P:(k + 1) * P], ident[:, :])
                mm.then_inc(s_mp, 1)
                pe.wait_ge(s_md, b * MD + MD_DG)
                for k in range(KT):
                    mm = pe.matmul(psM[:, k * P:(k + 1) * P], ones[:, :], dg[:, k, :], start=True, stop=True)
                mm.then_inc(s_mp, 1)
                for r in range(JT):
                    if r % 4 == 0:
                        pe.wait_ge(s_ma, b * MA + r // 4 + 1)
                    for k in range(KT):
                        mm = pe.matmul(psS[:, k, 0:DIM + 1], LG[:, r, k * P:(k + 1) * P], XN[:, r, :],
                                       start=r == 0, stop=r == JT - 1)
                mm.then_inc(s_mp, 1)
                pe.wait_ge(s_md, b * MD + MD_SI)
                for k in range(KT):
                    for h in range(KT):
                        o0 = h * ES + k * P
                        mm = pe.transpose(psS[:, 2, o0:o0 + P], si[:, k, h * P:(h + 1) * P], ident[:, :])
                mm.then_inc(s_mp, 1)
                pe.wait_ge(s_md, b * MD + MD_SIT)
                for e in range(E):
                    e2, a_ = e % 2, e // 2
                    for k in range(KT):
                        mm = pe.matmul(psS[e2 * HID:(e2 + 1) * HID, 3, a_ * S:(a_ + 1) * S],
                                       w1_s[:, k, e, :], siT[:, k, e * S:(e + 1) * S],
                                       start=k == 0, stop=k == KT - 1)
                mm.then_inc(s_mp, 1)
                pe.wait_ge(s_ma, b * MA + MA)
                for a_ in range(EP):
                    w = a_ % 4
                    mm = pe.matmul(psP[32 * w:32 * w + 32, a_ // 4, 0:DIM], HDg[:, a_, :], w2_s[:, a_, :],
                                   start=True, stop=True)
                mm.then_inc(s_mp, 1)
                pe.wait_ge(s_md, b * MD + MD_SO)
                pe.wait_ge(s_ldc, b * 64 + 64)
                for r in range(JT):
                    if r >= 4:
                        pe.wait_ge(s_md, b * MD + MD_ROW + 2 * (r - 4) + 1)
                    for k in range(KT):
                        mm = pe.matmul(psS[:, r % 4, 0:DIM], CT[:, r, k * P:(k + 1) * P], SO[:, k, :],
                                       start=k == 0, stop=k == KT - 1)
                    mm.then_inc(s_mp, 1)
                barrier(pe, b * MEET + 4)


def _tables():
    inv = (1.0 / np.float32(10000.0) ** (np.arange(0, HD, 2, dtype=np.float32) / np.float32(HD))).astype(np.float32)
    freqs = np.arange(N, dtype=np.float32)[:, None] * inv[None, :]
    both = []
    for f in (np.cos, np.sin):
        t = f(freqs.astype(np.float64)).astype(np.float32).T
        both.append(np.ascontiguousarray(np.tile(t, (H, 1))))
    return both


def kernel(**inputs):
    import concourse.bacc as bacc
    from concourse.bass_utils import run_bass_kernel_spmd as run

    a = {k[3:]: np.asarray(v) for k, v in inputs.items()}
    wq = a["attn_Wqkv"]
    order = (np.arange(H)[:, None] * HD + np.arange(HALF)[None, :]).reshape(-1)
    rows = np.concatenate([order, order + HALF, DIM + order, DIM + order + HALF])

    def halves(m):
        return m.reshape(KT, P, -1).transpose(1, 0, 2)

    def wide(v):
        return np.broadcast_to(v.reshape(1, -1), (P, v.size))

    cos_t, sin_t = _tables()
    wo = np.tile(a["attn_Wout"].T.reshape(GQ, 4, 1, HD, DIM).transpose(1, 2, 3, 0, 4), (1, 2, 1, 1, 1))
    wo = wo.reshape(P, GQ, DIM)
    arrays = dict(
        x=a["attn_x"].reshape(B, NIT, P, DIM),
        xT=a["attn_x"].transpose(0, 2, 1).reshape(B, KT, P, N).transpose(0, 2, 1, 3),
        wqk=halves(wq[rows].T), wv=halves(wq[2 * DIM:].T),
        bqk=a["attn_bqkv"][rows].reshape(4, P).T, bv=wide(a["attn_bqkv"][2 * DIM:]),
        wpre=np.repeat(a["attn_Wpre"].T, HALF, axis=0), wpost=np.repeat(a["attn_Wpost"].T, QI, axis=0),
        imask=np.tile(np.eye(QI, dtype=np.float32), (H, 1)),
        wout=wo, bout=wide(a["attn_bout"]), gamma=wide(a["ffn_ln_gamma"]), beta=wide(a["ffn_ln_beta"]),
        mu=halves(a["ffn_mu"].reshape(DIM, ES)), scale=wide(a["ffn_scale"]),
        w1=a["ffn_w1"].transpose(1, 0, 2).reshape(KT, P, E, HID).transpose(1, 0, 2, 3),
        b1=a["ffn_b1"].reshape(EP, P).T, w2=a["ffn_w2"].reshape(EP, P, DIM).transpose(1, 0, 2),
        b2=halves(np.repeat(a["ffn_b2"], S, axis=0)),
        cos_t=cos_t, sin_t=sin_t, ident_d=np.eye(P, dtype=np.float32),
    )
    arrays = {k: np.ascontiguousarray(v) for k, v in arrays.items()}
    nc = bacc.Bacc("TRN2", target_bir_lowering=False, num_devices=1)
    args = {k: nc.dram_tensor("in_" + k, v.shape, F32, kind="ExternalInput").ap() for k, v in arrays.items()}
    out = nc.dram_tensor("out_0", (B, NIT, P, DIM), F32, kind="ExternalOutput").ap()
    seq_layer(nc, out=out, **args)
    r = run(nc, [{"in_" + k: v for k, v in arrays.items()}], core_ids=[0])
    return r.results[0]["out_0"].reshape(B, N, DIM)
```
